# Optimizing a Trainium2 kernel written in Bass

```python
import numpy as np
import jax
import jax.numpy as jnp

def _softmax(x, axis=-1):
    return jax.nn.softmax(x, axis=axis)

def _gelu(x):
    return jax.nn.gelu(x, approximate=True)

def _silu(x):
    return jax.nn.silu(x)

def _sigmoid(x):
    return jax.nn.sigmoid(x)

def _layernorm(x, axis=-1, eps=1e-05):
    m = jnp.mean(x, axis=axis, keepdims=True)
    v = jnp.var(x, axis=axis, keepdims=True)
    return (x - m) / jnp.sqrt(v + eps)

def _scatter_add(tgt, idx, src, axis=0):
    return tgt.at[idx].add(src)

def _segment_sum(src, seg, n):
    return jax.ops.segment_sum(src, seg, n)
kernel_name = 'mk_xattn_seq_d2_seqx_r4_bbbf6b'

def setup_inputs(seed: int=0):
    np.random.seed(seed)
    _w = jnp.asarray

    def _rec_inputs():
        import jax
        import jax.numpy as jnp
        _rk = jax.random.key(seed)
        x = 7.22e-05 + 1 * jax.random.normal(jax.random.fold_in(_rk, 1), (16, 100, 512), jnp.float32)
        _lenS = 100 - jax.random.randint(jax.random.fold_in(_rk, 7), (16,), 0, max(1, 100 // 4) + 1, jnp.int32)
        _lenS2 = 361 - jax.random.randint(jax.random.fold_in(_rk, 8), (16,), 0, max(1, 361 // 4) + 1, jnp.int32)
        _ctx_2048P = jax.random.normal(jax.random.fold_in(_rk, 11), (16, 16, 512), jnp.float32)
        _ctx_2048c = jax.random.dirichlet(jax.random.fold_in(_rk, 511), 0.3 * jnp.ones((16,), jnp.float32), (16, 361))
        _ctx_2048t = jnp.einsum('bsk,bkd->bsd', _ctx_2048c, _ctx_2048P)
        _ctx_2048t = _ctx_2048t * jax.lax.rsqrt(jnp.mean(jnp.square(_ctx_2048t)) + 1e-12) * 0.953939
        ctx_2048 = 4.13588e-05 + 0.999923 * (_ctx_2048t + 0.3 * jax.random.normal(jax.random.fold_in(_rk, 611), (16, 361, 512), jnp.float32))
        _validS = jnp.arange(100)[None, :] < _lenS[:, None]
        _validS2 = jnp.arange(361)[None, :] < _lenS2[:, None]
        _causal = jnp.tril(jnp.ones((100, 100), dtype=bool))
        mask_Bx1xSxS2_ff0 = jnp.where(jnp.ones((16, 1, 100, 361), dtype=bool), 0.0, -1000000000.0).astype(jnp.float32)
        return (x, ctx_2048, mask_Bx1xSxS2_ff0)
    x, ctx_2048, mask_Bx1xSxS2_ff0 = _rec_inputs()

    def _L0_xattn_setup():
        import jax, jax.numpy as jnp
        import numpy as np
        H = 512
        NH = 32
        KVH = 8
        HD = H // NH
        GROUPS = NH // KVH
        EPS = 1e-06
        B, L, S = (4, 256, 256)

        def _gqa_forward(hidden_state, encoder_hidden_state, encoder_attention_mask, Wq, bq, Wk, bk, Wv, bv, Wo, bo, gamma, beta):
            b, l, _ = hidden_state.shape
            s = encoder_hidden_state.shape[1]
            q = hidden_state @ Wq + bq
            k = encoder_hidden_state @ Wk + bk
            v = encoder_hidden_state @ Wv + bv
            q = q.reshape(b, l, KVH, GROUPS, HD).transpose(0, 2, 3, 1, 4)
            k = k.reshape(b, s, KVH, HD).transpose(0, 2, 1, 3)
            v = v.reshape(b, s, KVH, HD).transpose(0, 2, 1, 3)
            scale = 1.0 / jnp.sqrt(jnp.asarray(HD, q.dtype))
            scores = jnp.einsum('bkgld,bksd->bkgls', q, k) * scale
            scores = scores + encoder_attention_mask[:, :, None, :, :]
            attn = jax.nn.softmax(scores, axis=-1)
            out = jnp.einsum('bkgls,bksd->bkgld', attn, v)
            out = out.transpose(0, 3, 1, 2, 4).reshape(b, l, H)
            out = out @ Wo + bo
            x = out + hidden_state
            mu = jnp.mean(x, axis=-1, keepdims=True)
            var = jnp.var(x, axis=-1, keepdims=True)
            return (x - mu) * jax.lax.rsqrt(var + EPS) * gamma + beta
        key = jax.random.key(seed)
        ks = jax.random.split(key, 12)
        sd = 0.02
        return {'hidden_state': jax.random.normal(ks[0], (B, L, H), jnp.float32), 'encoder_hidden_state': jax.random.normal(ks[1], (B, S, H), jnp.float32), 'encoder_attention_mask': jnp.zeros((B, 1, L, S), jnp.float32), 'Wq': jax.random.normal(ks[2], (H, H), jnp.float32) * sd, 'bq': jnp.zeros((H,), jnp.float32), 'Wk': jax.random.normal(ks[3], (H, KVH * HD), jnp.float32) * sd, 'bk': jnp.zeros((KVH * HD,), jnp.float32), 'Wv': jax.random.normal(ks[4], (H, KVH * HD), jnp.float32) * sd, 'bv': jnp.zeros((KVH * HD,), jnp.float32), 'Wo': jax.random.normal(ks[5], (H, H), jnp.float32) * sd, 'bo': jnp.zeros((H,), jnp.float32), 'gamma': jnp.ones((H,), jnp.float32), 'beta': jnp.zeros((H,), jnp.float32)}
    _L0_xattn_all = _L0_xattn_setup()
    _L0_xattn_in = {k: v for k, v in _L0_xattn_all.items() if k in ('Wq', 'bq', 'Wk', 'bk', 'Wv', 'bv', 'Wo', 'bo', 'gamma', 'beta')}
    del _L0_xattn_all

    def _L1_xattn_setup():
        import jax, jax.numpy as jnp
        import numpy as np
        H = 512
        B, L, S = (4, 1024, 10)
        key = jax.random.key(seed)
        k1, k2, k3, k4, k5, k6 = jax.random.split(key, 6)
        scale = 1.0 / np.sqrt(H)
        return {'h_english': jax.random.normal(k1, (B, L, H), dtype=jnp.float32), 'h_lojban': jax.random.normal(k2, (B, S, H), dtype=jnp.float32), 'w_q': jax.random.normal(k3, (H, H), dtype=jnp.float32) * scale, 'w_k': jax.random.normal(k4, (H, H), dtype=jnp.float32) * scale, 'w_v': jax.random.normal(k5, (H, H), dtype=jnp.float32) * scale, 'w_o': jax.random.normal(k6, (H, H), dtype=jnp.float32) * scale, 'alpha': jnp.float32(0.1)}
    _L1_xattn_all = _L1_xattn_setup()
    _L1_xattn_in = {k: v for k, v in _L1_xattn_all.items() if k in ('w_q', 'w_k', 'w_v', 'w_o', 'alpha')}
    del _L1_xattn_all
    return {'x': x, 'ctx_2048': ctx_2048, 'mask_Bx1xSxS2_ff0': mask_Bx1xSxS2_ff0, 'L0_xattn_Wq': _L0_xattn_in['Wq'], 'L0_xattn_bq': _L0_xattn_in['bq'], 'L0_xattn_Wk': _L0_xattn_in['Wk'], 'L0_xattn_bk': _L0_xattn_in['bk'], 'L0_xattn_Wv': _L0_xattn_in['Wv'], 'L0_xattn_bv': _L0_xattn_in['bv'], 'L0_xattn_Wo': _L0_xattn_in['Wo'], 'L0_xattn_bo': _L0_xattn_in['bo'], 'L0_xattn_gamma': _L0_xattn_in['gamma'], 'L0_xattn_beta': _L0_xattn_in['beta'], 'L1_xattn_w_q': _L1_xattn_in['w_q'], 'L1_xattn_w_k': _L1_xattn_in['w_k'], 'L1_xattn_w_v': _L1_xattn_in['w_v'], 'L1_xattn_w_o': _L1_xattn_in['w_o'], 'L1_xattn_alpha': _L1_xattn_in['alpha']}

def reference(x, ctx_2048, mask_Bx1xSxS2_ff0, L0_xattn_Wq, L0_xattn_bq, L0_xattn_Wk, L0_xattn_bk, L0_xattn_Wv, L0_xattn_bv, L0_xattn_Wo, L0_xattn_bo, L0_xattn_gamma, L0_xattn_beta, L1_xattn_w_q, L1_xattn_w_k, L1_xattn_w_v, L1_xattn_w_o, L1_xattn_alpha):
    import jax
    import jax.numpy as jnp

    def _L0_xattn_ref(hidden_state, encoder_hidden_state, encoder_attention_mask, Wq, bq, Wk, bk, Wv, bv, Wo, bo, gamma, beta):
        import jax, jax.numpy as jnp
        import numpy as np
        H = 512
        NH = 32
        KVH = 8
        HD = H // NH
        GROUPS = NH // KVH
        EPS = 1e-06
        B, L, S = (4, 256, 256)

        def _gqa_forward(hidden_state, encoder_hidden_state, encoder_attention_mask, Wq, bq, Wk, bk, Wv, bv, Wo, bo, gamma, beta):
            b, l, _ = hidden_state.shape
            s = encoder_hidden_state.shape[1]
            q = hidden_state @ Wq + bq
            k = encoder_hidden_state @ Wk + bk
            v = encoder_hidden_state @ Wv + bv
            q = q.reshape(b, l, KVH, GROUPS, HD).transpose(0, 2, 3, 1, 4)
            k = k.reshape(b, s, KVH, HD).transpose(0, 2, 1, 3)
            v = v.reshape(b, s, KVH, HD).transpose(0, 2, 1, 3)
            scale = 1.0 / jnp.sqrt(jnp.asarray(HD, q.dtype))
            scores = jnp.einsum('bkgld,bksd->bkgls', q, k) * scale
            scores = scores + encoder_attention_mask[:, :, None, :, :]
            attn = jax.nn.softmax(scores, axis=-1)
            out = jnp.einsum('bkgls,bksd->bkgld', attn, v)
            out = out.transpose(0, 3, 1, 2, 4).reshape(b, l, H)
            out = out @ Wo + bo
            x = out + hidden_state
            mu = jnp.mean(x, axis=-1, keepdims=True)
            var = jnp.var(x, axis=-1, keepdims=True)
            return (x - mu) * jax.lax.rsqrt(var + EPS) * gamma + beta
        return _gqa_forward(hidden_state, encoder_hidden_state, encoder_attention_mask, Wq, bq, Wk, bk, Wv, bv, Wo, bo, gamma, beta)

    def _L1_xattn_ref(h_english, h_lojban, w_q, w_k, w_v, w_o, alpha):
        import jax, jax.numpy as jnp
        import numpy as np
        H = 512
        B, L, S = (4, 1024, 10)
        h = h_english.shape[-1]
        q = jnp.einsum('blh,oh->blo', h_english, w_q)
        k = jnp.einsum('bsh,oh->bso', h_lojban, w_k)
        v = jnp.einsum('bsh,oh->bso', h_lojban, w_v)
        scores = jnp.einsum('blh,bsh->bls', q, k) / jnp.sqrt(jnp.float32(h))
        probs = jax.nn.softmax(scores, axis=-1)
        context = jnp.einsum('bls,bsh->blh', probs, v)
        delta = jnp.einsum('blh,oh->blo', context, w_o)
        return h_english + alpha * delta
    x = _L0_xattn_ref(x, ctx_2048, mask_Bx1xSxS2_ff0, L0_xattn_Wq, L0_xattn_bq, L0_xattn_Wk, L0_xattn_bk, L0_xattn_Wv, L0_xattn_bv, L0_xattn_Wo, L0_xattn_bo, L0_xattn_gamma, L0_xattn_beta)
    x = _L1_xattn_ref(x, ctx_2048, L1_xattn_w_q, L1_xattn_w_k, L1_xattn_w_v, L1_xattn_w_o, L1_xattn_alpha)
    return x

_drawn_inputs = setup_inputs


def setup_inputs(seed=0):
    import zlib

    import numpy as np

    out = dict(_drawn_inputs(seed))
    spreads = {'L0_xattn_bq': (0.0, 0.8),
     'L0_xattn_bk': (0.0, 0.8),
     'L0_xattn_bv': (0.0, 0.1),
     'L0_xattn_bo': (0.0, 0.1),
     'L0_xattn_gamma': (1.0, 0.2),
     'L0_xattn_beta': (0.0, 0.1)}
    factors = {'L0_xattn_Wq': 7.63, 'L0_xattn_Wk': 7.467, 'L1_xattn_w_q': 2.81, 'L1_xattn_w_k': 2.858}
    for name, (base, spread) in spreads.items():
        noise = np.random.default_rng([zlib.crc32(name.encode()), seed]).standard_normal(out[name].shape)
        drawn = base * np.exp(spread * noise) if base else spread * noise
        out[name] = jnp.asarray(drawn.astype(out[name].dtype))
    for name, factor in factors.items():
        out[name] = (out[name] * factor).astype(out[name].dtype)
    return out
```

```python
from contextlib import ExitStack

import concourse.bass as bass
from concourse import mybir

F32 = mybir.dt.float32
F32R = mybir.dt.float32r
ACT = mybir.ActivationFunctionType
ALU = mybir.AluOpType
AX = mybir.AxisListType

B, L, S, H = 16, 100, 361, 512
NH, KVH, HD = 32, 8, 16
J = NH // KVH
P = 128
KT = H // P
SP2 = S + 1
SC = 3
LAST = S - 2 * P
JL = J * L
EPS = 1e-6

LOOP = (2, 14)
STEPS = (-2, B + 2)

BANK_USERS = (
    (("p1t", -2, "p1t_ok", 2, 2), ("cx", -2, "cxt_ok", 1, 1), ("d", -2, "res_ok", 1, 1), ("c1", 0, "ml_ok", 2, 2),
     ("vt", 1, "va_ok", 2, 2), ("x1t", -1, "x1l_ok", 1, 1), ("xmt", -1, "xmt_ok", 1, 1), ("s1", -1, "p1_ok", 1, 1)),
    (("q", 1, "q_nat", 1, 1), ("k", 1, "kl_ok", 1, 1), ("qt", 1, "ql_ok", 1, 1), ("v", 1, "vT_ok", 1, 1),
     ("y", -1, "y_ok", 1, 1), ("xm", -1, "xm_ok", 1, 1), ("c0", 1, "ml_ok", 2, 1)),
)


def in_range(batch):
    return 0 <= batch < B


def upto(count):
    return min(count, B) if isinstance(count, int) else count


def emptied(bank, piece, i):
    users = BANK_USERS[bank]
    at = [user[0] for user in users].index(piece)
    for back in range(1, 3 * len(users)):
        behind, before = divmod(at - back, len(users))
        _, off, name, each, done = users[before]
        batch = i + behind + off
        if not isinstance(i, int) or in_range(batch):
            return name, each * batch + done
    return None, 0


def wait(eng, sem, value):
    if not (isinstance(value, int) and value <= 0):
        eng.wait_ge(sem, value)


def hold(eng, sem, value):
    wait(eng, sem, value)
    if not isinstance(value, int):
        eng.nop(nofuse=True)


def ring(b, par, dmas=1):
    return (8 * b - 8 * par + 16) * dmas


def run_steps(nc, eng, body):
    for i in range(STEPS[0], LOOP[0]):
        body(i, i % 2, lambda off, i=i: in_range(i + off))
    with eng.Fori(LOOP[0], LOOP[1], 2) as i:
        i = nc.s_assert_within(i, LOOP[0], LOOP[1] - 2,
                               skip_runtime_bounds_check_because="the loop goes by two and its range is even")
        body(i, 0, lambda off: True)
        body(i + 1, 1, lambda off: True)
    for i in range(LOOP[1], STEPS[1]):
        body(i, i % 2, lambda off, i=i: in_range(i + off))


def build(nc, xT_d, x_d, ctxT_d, ctx_d, mask_d, maskT_d, wq_d, wk_d, wv_d, wo_d, bq_d, bk_d, bv_d,
          bo_d, gamma_d, beta_d, w1q_d, w1k_d, w1v_d, w1o_d, alpha_d, out_d):
    with ExitStack() as ctx:
        def sb(name, shape, dt=F32):
            return ctx.enter_context(nc.sbuf_tensor(name, shape, dt))

        def sem(name):
            return ctx.enter_context(nc.semaphore(name))

        sc_ps = ctx.enter_context(nc.psum_tensor("sc_ps", [P, SC, 512], F32))
        mx_ps = ctx.enter_context(nc.psum_tensor("mx_ps", [P, 2, 512], F32))
        o_ps = ctx.enter_context(nc.psum_tensor("o_ps", [P, 512], F32))
        work = ctx.enter_context(nc.psum_tensor("work", [P, 2, 512], F32))

        wq_h, wq_l = sb("wq_h", [P, KT, H], F32R), sb("wq_l", [P, KT, H], F32R)
        wk_h, wk_l = sb("wk_h", [P, KT, P], F32R), sb("wk_l", [P, KT, P], F32R)
        wv_h, wv_l = sb("wv_h", [P, KT, P], F32R), sb("wv_l", [P, KT, P], F32R)
        m_h, m_l = sb("m_h", [P, KT, H], F32R), sb("m_l", [P, KT, H], F32R)
        n_w = sb("n_w", [P, KT, H])
        wo_w = sb("wo_w", [P, J, H])
        bq_b, gamma_b, beta_b, bo_b = (sb(n, [L, H]) for n in ("bq_b", "gamma_b", "beta_b", "bo_b"))
        bk_c, bv_c = sb("bk_c", [P, 1]), sb("bv_c", [P, 1])
        bo_r = sb("bo_r", [1, H])
        alpha_c = sb("alpha_c", [L, 1])
        half_c = sb("half_c", [L, 1])
        ident = sb("ident", [P, P])
        ones = sb("ones", [P, L])
        bv_b = sb("bv_b", [P, L])

        xT = [sb(f"xT{p}", [P, KT * L]) for p in range(2)]
        cT = sb("cT", [P, KT * SP2])
        x_h, x_l = sb("x_h", [P, JL], F32R), sb("x_l", [P, JL], F32R)
        c_h, c_l = sb("c_h", [P, KT * SP2], F32R), sb("c_l", [P, KT * SP2], F32R)
        q_n = sb("q_n", [L, H])
        q_h, q_l = sb("q_h", [P, JL], F32R), sb("q_l", [P, JL], F32R)
        k_h, k_l = sb("k_h", [P, SP2], F32R), sb("k_l", [P, SP2], F32R)
        vT = sb("vT", [P, SP2])
        va = [sb(f"va{p}", [P, SC, KVH, 2 * HD]) for p in range(2)]
        qs = [sb(f"qs{p}", [66, KVH, JL], F32R) for p in range(2)]
        ks = [sb(f"ks{p}", [66, KVH, SC * P], F32R) for p in range(2)]
        mask_n = sb("mask_n", [L, S])
        mx = [sb(f"mx{p}", [L, NH]) for p in range(2)]
        mt_h = [sb(f"mt_h{h}", [NH // 2, L], F32R) for h in range(2)]
        mt_l = [sb(f"mt_l{h}", [NH // 2, L], F32R) for h in range(2)]

        mask_t = [sb(f"mask_t{p}", [P, SC, L]) for p in range(2)]
        pr = sb("pr", [P, 4, SC, JL])
        o_s = [sb(f"o_s{h}", [P, JL]) for h in range(2)]

        o_n, r_b = sb("o_n", [P, JL]), sb("r_b", [P, JL])
        den, rden = sb("den", [NH, L]), sb("rden", [NH, L])
        y = sb("y", [L, H])
        stats, mv, ve, rstd = sb("stats", [L, 6]), sb("mv", [L, 2]), sb("ve", [L, 1]), sb("rstd", [L, 1])
        x1 = [sb(f"x1_{p}", [L, H]) for p in range(2)]
        xm_n = sb("xm_n", [L, H])
        nm1, s1, ra0, ra = sb("nm1", [L, 1]), sb("s1", [L, 1]), sb("ra0", [L, 1]), sb("ra", [L, 1])
        p1, p1_t = sb("p1", [L, SP2]), sb("p1_t", [P, SC, L])
        ctx_n = sb("ctx_n", [P, SC, H])
        turned = sb("turned", [P, JL])

        k_dr = nc.dram_tensor("k_dr", (2, 2, P, SP2), F32, kind="Internal").ap()
        q_dr = nc.dram_tensor("q_dr", (2, 2, P, JL), F32, kind="Internal").ap()
        o_dr = nc.dram_tensor("o_dr", (2, KVH * 32, JL), F32, kind="Internal").ap()
        r_dr = nc.dram_tensor("r_dr", (NH, L), F32, kind="Internal").ap()

        w_in = [sem(f"w_in{n}") for n in range(5)]
        prep_act, prep_dve, prep_pool, prep_pe = sem("prep_act"), sem("prep_dve"), sem("prep_pool"), sem("prep_pe")
        x_in = [sem(f"x_in{p}") for p in range(2)]
        c_in = sem("c_in")
        c4_in = sem("c4_in")
        xh_ok, xl_ok, ch_ok, cl_ok = (sem(n) for n in ("xh_ok", "xl_ok", "ch_ok", "cl_ok"))
        q_mm, q_nat, q_tr, qh_ok, ql_ok = (sem(n) for n in ("q_mm", "q_nat", "q_tr", "qh_ok", "ql_ok"))
        k_mm, kh_ok, kl_ok = sem("k_mm"), sem("kh_ok"), sem("kl_ok")
        v_mm, vT_ok, v_tr, va_ok = sem("v_mm"), sem("vT_ok"), sem("v_tr"), sem("va_ok")
        k_out, q_out = sem("k_out"), sem("q_out")
        ks_in, qs_in = sem("ks_in"), sem("qs_in")
        mn_in = sem("mn_in")
        mt_in = [sem(f"mt_in{p}") for p in range(2)]
        a_mm, a_mx = sem("a_mm"), sem("a_mx")
        m_tr, mh_ok, ml_ok = sem("m_tr"), sem("mh_ok"), sem("ml_ok")
        m_in = [sem(f"m_in{h}") for h in range(2)]
        sc_mm = sem("sc_mm")
        sc_add, sc_cp, sc_pool = sem("sc_add"), sem("sc_cp"), sem("sc_pool")
        ex_ok = sem("ex_ok")
        pv_mm, os_ok = sem("pv_mm"), sem("os_ok")
        os_out = [sem(f"os_out{h}") for h in range(2)]
        ot_in, rd_ok, rd_out, rb_in = sem("ot_in"), sem("rd_ok"), sem("rd_out"), sem("rb_in")
        on_ok = sem("on_ok")
        xn_in, xb_ok = sem("xn_in"), sem("xb_ok")
        y_mm, y_ok, st_ok, mv_ok, ve_ok, rstd_ok, xc_ok, xg_ok, x1_ok = (
            sem(n) for n in ("y_mm", "y_ok", "st_ok", "mv_ok", "ve_ok", "rstd_ok", "xc_ok", "xg_ok", "x1_ok"))
        x1_tr, x1h_ok, x1l_ok = sem("x1_tr"), sem("x1h_ok"), sem("x1l_ok")
        xm_mm, xm_ok, xm_tr, xmt_ok = sem("xm_mm"), sem("xm_ok"), sem("xm_tr"), sem("xmt_ok")
        s1_mm, nm_ok, p1_ok, ra0_ok, ra_ok = (sem(n) for n in ("s1_mm", "nm_ok", "p1_ok", "ra0_ok", "ra_ok"))
        p1_tr, p1t_ok, cn_in, cx_mm, cxt_ok = (sem(n) for n in ("p1_tr", "p1t_ok", "cn_in", "cx_mm", "cxt_ok"))
        d_mm, res_ok = sem("d_mm"), sem("res_ok")
        out_ok = [sem(f"out_ok{p}") for p in range(2)]

        block = ctx.enter_context(nc.Block())

        @block.sync
        def _(sp):
            st = pr[:, :, :, :].rearrange("p a b c -> p (a b c)")
            sp.dma_start(st[:, 0:2048], wq_d).then_inc(w_in[0], 16)
            sp.dma_start(st[:, 2048:2560], wk_d).then_inc(w_in[0], 16)
            sp.dma_start(st[:, 2560:3072], wv_d).then_inc(w_in[0], 16)
            sp.dma_start(wo_w[:, :, :].rearrange("p a b -> p (a b)"), wo_d).then_inc(w_in[1], 16)
            sp.dma_start(bq_b[:, :], bq_d).then_inc(w_in[1], 16)
            sp.dma_start(gamma_b[:, :], gamma_d).then_inc(w_in[1], 16)
            sp.dma_start(beta_b[:, :], beta_d).then_inc(w_in[1], 16)
            sp.dma_start(bk_c[:, :], bk_d).then_inc(w_in[1], 16)
            sp.dma_start(bv_c[:, :], bv_d).then_inc(w_in[1], 16)
            sp.dma_start(bo_r[:, :], bo_d).then_inc(w_in[1], 16)
            sp.dma_start(alpha_c[:, :], alpha_d).then_inc(w_in[1], 16)
            sp.wait_ge(prep_act, 3)
            sp.wait_ge(prep_dve, 3)
            sp.dma_start(st[:, 0:2048], w1q_d).then_inc(w_in[2], 16)
            sp.dma_start(st[:, 2048:4096], w1k_d).then_inc(w_in[2], 16)
            sp.wait_ge(prep_pe, 5)
            sp.dma_start(st[:, 0:2048], w1v_d).then_inc(w_in[3], 16)
            sp.dma_start(st[:, 2048:4096], w1o_d).then_inc(w_in[3], 16)

            def step(i, par, has):
                odd = 1 - par
                if has(2):
                    b = i + 2
                    hold(sp, xh_ok, i + 1)
                    hold(sp, xl_ok, i + 1)
                    sp.dma_start(xT[par][:, :], xT_d[b, :, :]).then_inc(x_in[par], 16)
                if has(1):
                    b = i + 1
                    hold(sp, ch_ok, i + 1)
                    hold(sp, cl_ok, i + 1)
                    hold(sp, s1_mm, i - 1)
                    sp.dma_start(cT[:, :], ctxT_d[b, :, :]).then_inc(c_in, 16)
                if has(1):
                    b = i + 1
                    hold(sp, a_mx, NH * b)
                    sp.dma_start(mask_n[:, :], mask_d[b, :, :]).then_inc(mn_in, 16)
                if has(-1):
                    b = i - 1
                    hold(sp, os_ok, 2 * b + 2)
                    sp.dma_start(o_dr[odd, P:2 * P, :], o_s[1][:, :]).then_inc(os_out[1], 16)
                if has(1):
                    b = i + 1
                    hold(sp, sc_add, 16 * i)
                    hold(sp, sc_pool, 8 * i)
                    sp.dma_start(mask_t[odd][:, :, :], maskT_d[b, :, :, :]).then_inc(mt_in[odd], 16)
                    hold(sp, kh_ok, b + 1)
                    hold(sp, kl_ok, b + 1)
                    hold(sp, ks_in, 64 * i)
                    sp.dma_start(k_dr[odd, 0, :, :], k_h[:, :].bitcast(F32)).then_inc(k_out, 16)
                    sp.dma_start(k_dr[odd, 1, :, :], k_l[:, :].bitcast(F32)).then_inc(k_out, 16)
                if has(-1):
                    b = i - 1
                    hold(sp, os_out[0], 16 * (b + 1))
                    hold(sp, os_out[1], 16 * (b + 1))
                    hold(sp, y_mm, b)
                    hold(sp, rd_ok, b)
                    rows = o_dr[odd, :, :].rearrange("(g r) c -> g r c", r=2 * HD)
                    sp.dma_start(o_n[:, :], rows[:, 0:HD, :]).then_inc(ot_in, 16)
                    sp.dma_start(den[:, :], rows[:, HD, :].rearrange("g (j l) -> g j l", j=J)).then_inc(ot_in, 16)
                if has(1):
                    b = i + 1
                    hold(sp, k_out, 32 * (b + 1))
                    hold(sp, sc_mm, 24 * i)
                    for r in range(4):
                        sp.dma_start(ks[odd][HD * r:HD * (r + 1), :, 0:SP2].bitcast(F32),
                                     k_dr[odd, r // 2, :, :].rearrange("(g d) s -> d g s", d=HD)).then_inc(ks_in, 16)
                if has(-1):
                    b = i - 1
                    hold(sp, ch_ok, upto(i + 2))
                    hold(sp, cl_ok, upto(i + 2))
                    hold(sp, s1_mm, b)
                    sp.dma_start(cT[:, :], ctxT_d[b, :, :]).then_inc(c4_in, 16)
                    hold(sp, xg_ok, b)
                    sp.dma_start(y[:, :], x_d[b, :, :]).then_inc(xn_in, 16)
                    hold(sp, cx_mm, b)
                    sp.dma_start(ctx_n[:, :, :], ctx_d[b, :, :, :]).then_inc(cn_in, 16)
                if has(-2):
                    b = i - 2
                    hold(sp, res_ok, b + 1)
                    sp.dma_start(out_d[b, :, :], x1[par][:, :]).then_inc(out_ok[par], 16)
                if has(1):
                    b = i + 1
                    hold(sp, qh_ok, b + 1)
                    hold(sp, ql_ok, b + 1)
                    hold(sp, qs_in, 64 * i)
                    sp.dma_start(q_dr[odd, 0, :, :], q_h[:, :].bitcast(F32)).then_inc(q_out, 16)
                    sp.dma_start(q_dr[odd, 1, :, :], q_l[:, :].bitcast(F32)).then_inc(q_out, 16)
                    hold(sp, q_out, 32 * (b + 1))
                    for r in range(4):
                        sp.dma_start(qs[odd][HD * r:HD * (r + 1), :, :].bitcast(F32),
                                     q_dr[odd, r % 2, :, :].rearrange("(g d) c -> d g c", d=HD)).then_inc(qs_in, 16)

                def maxima_in(b, half, stack):
                    hold(sp, mh_ok, 2 * b + half + 1)
                    hold(sp, ml_ok, 2 * b + half + 1)
                    for row, t in ((64, mt_h[half]), (65, mt_l[half])):
                        dst = stack[row:row + 1, 4 * half:4 * half + 4, :].bitcast(F32).rearrange("p g (j l) -> p (g j) l", j=J)
                        sp.dma_start(dst, t[:, :].bitcast(F32)).then_inc(m_in[half], 16)

                if has(0):
                    maxima_in(i, 1, qs[par])
                if has(-1):
                    b = i - 1
                    hold(sp, rd_ok, b + 1)
                    hold(sp, rb_in, 16 * b)
                    sp.dma_start(r_dr[:, :], rden[:, :]).then_inc(rd_out, 16)
                    hold(sp, rd_out, 16 * (b + 1))
                    src = r_dr[:, :].rearrange("(g j) l -> g (j l)", j=J).unsqueeze(1).to_broadcast([KVH, HD, JL])
                    sp.dma_start(r_b[:, :], src).then_inc(rb_in, 16)
                if has(0):
                    hold(sp, os_ok, 2 * i + 1)
                    hold(sp, ot_in, 32 * (i - 1))
                    sp.dma_start(o_dr[par, 0:P, :], o_s[0][:, :]).then_inc(os_out[0], 16)
                if has(1):
                    maxima_in(i + 1, 0, qs[odd])

            run_steps(nc, sp, step)
            for p in range(2):
                sp.wait_ge(out_ok[p], 16 * (B // 2))

        @block.tensor
        def _(pe):
            bank_read = dict(p1t_ok=p1t_ok, cxt_ok=cxt_ok, res_ok=res_ok, ml_ok=ml_ok, va_ok=va_ok, x1l_ok=x1l_ok,
                             xmt_ok=xmt_ok, p1_ok=p1_ok, q_nat=q_nat, kl_ok=kl_ok, ql_ok=ql_ok, vT_ok=vT_ok,
                             y_ok=y_ok, xm_ok=xm_ok)
            st = pr[:, :, :, :].rearrange("p a b c -> p (a b c)")
            pe.wait_ge(w_in[1], 128)
            pe.wait_ge(prep_dve, 5)
            pe.wait_ge(prep_pool, 9)
            for j in range(J):
                nc.tensor.matmul(o_ps[0:L, :], bv_b[:, :], wo_w[:, j, :], start=(j == 0), stop=False)
            nc.tensor.matmul(o_ps[0:L, :], ones[0:1, :], bo_r[:, :], start=False, stop=True).then_inc(prep_pe, 1)
            for n in range(2):
                pe.wait_ge(w_in[2 + n], 32)
                for t in range(KT):
                    dst = sc_ps[:, t, :] if t < SC else mx_ps[:, 0, :]
                    if n == 1:
                        pe.wait_ge(prep_act, 3 + t + 1)
                        pe.wait_ge(prep_dve, 5 + t + 1)
                    for o in range(KT):
                        mm = nc.tensor.matmul(dst, st[:, 512 * o + P * t:512 * o + P * (t + 1)],
                                              st[:, 2048 + 512 * o:2048 + 512 * (o + 1)],
                                              start=(o == 0), stop=(o == KT - 1))
                    mm.then_inc(prep_pe, 1)
            pe.wait_ge(prep_act, 11)
            pe.wait_ge(prep_dve, 10)

            def product(dst, lh, ll, rh, rl, k, last):
                nc.tensor.matmul(dst, lh, rh, start=(k == 0), stop=False)
                nc.tensor.matmul(dst, lh, rl, start=False, stop=False)
                return nc.tensor.matmul(dst, ll, rh, start=False, stop=(k == last))

            def step(i, par, has):
                odd = 1 - par

                def bank(w, piece):
                    name, count = emptied(w, piece, i)
                    wait(pe, bank_read.get(name), count)
                    return work[:, w, :]

                def scores(g):
                    if not has(0):
                        return
                    b = i
                    if g == 0:
                        pe.wait_ge(m_in[0], 32 * (b + 1))
                    if g == KVH // 2:
                        pe.wait_ge(m_in[1], 32 * (b + 1))
                    for c in range(SC):
                        if c < 2:
                            wait(pe, sc_add, 2 * (8 * b + g - 1) + c + 1)
                        else:
                            wait(pe, sc_cp, 8 * b + g)
                        nc.tensor.matmul(sc_ps[:, c, 0:JL], ks[par][:, g, P * c:P * (c + 1)], qs[par][:, g, :],
                                         start=True, stop=True).then_inc(sc_mm, 1)

                def heads(n0, n1):
                    if not has(1):
                        return
                    b = i + 1
                    for n in range(n0, n1):
                        g, j = n // J, n % J
                        if n == 0:
                            pe.wait_ge(ks_in, 64 * (b + 1))
                            pe.wait_ge(qs_in, 64 * (b + 1))
                        wait(pe, a_mx, NH * b + n - 1)
                        nc.tensor.matmul(mx_ps[0:L, n % 2, 0:SP2], qs[odd][0:64, g, L * j:L * (j + 1)],
                                         ks[odd][0:64, g, 0:SP2], start=True, stop=True).then_inc(a_mm, 1)

                def values(off, half):
                    if not has(off):
                        return
                    b, p = i + off, (par + off) % 2
                    pe.wait_ge(ex_ok, 8 * b + 4 * half + 4)
                    if half == 0:
                        pe.wait_ge(va_ok, 2 * (b + 1))
                    wait(pe, os_ok, 2 * b + half)
                    for c in range(SC):
                        k = P if c < 2 else LAST
                        for q in range(4):
                            mm = nc.tensor.matmul(o_ps[32 * q:32 * (q + 1), 0:JL], va[p][0:k, c, 4 * half + q, :],
                                                  pr[0:k, q, c, :], start=(c == 0), stop=(c == SC - 1))
                    mm.then_inc(pv_mm, 1)

                def turn_maxima(off, half, w, piece):
                    if not has(off):
                        return
                    b, p = i + off, (par + off) % 2
                    pe.wait_ge(a_mx, NH * b + 16 * (half + 1))
                    dst = bank(w, piece)
                    nc.tensor.matmul(dst[0:16, 0:L], mx[p][:, 16 * half:16 * half + 16], ident[0:L, 0:L],
                                     is_transpose=True, start=True, stop=True).then_inc(m_tr, 1)

                def turn4(w, piece, src, done):
                    dst = bank(w, piece)
                    for j in range(KT):
                        mm = nc.tensor.matmul(dst[:, L * j:L * (j + 1)], src(j), ident[0:L, 0:L],
                                              is_transpose=True, start=True, stop=True)
                    mm.then_inc(done, 1)

                scores(0)
                if has(-2):
                    b = i - 2
                    pe.wait_ge(p1_ok, b + 1)
                    dst = bank(0, "p1t")
                    for c in range(SC):
                        k = P if c < 2 else LAST
                        mm = nc.tensor.matmul(dst[0:k, L * c:L * (c + 1)], p1[:, P * c:P * c + k], ident[0:L, 0:L],
                                              is_transpose=True, start=True, stop=True)
                    mm.then_inc(p1_tr, 1)
                if has(1):
                    b = i + 1
                    pe.wait_ge(xh_ok, b + 1)
                    pe.wait_ge(xl_ok, b + 1)
                    dst = bank(1, "q")
                    for k in range(KT):
                        xs = slice(L * k, L * (k + 1))
                        mm = product(dst[0:L, :], x_h[:, xs], x_l[:, xs], wq_h[:, k, :], wq_l[:, k, :], k, KT - 1)
                    mm.then_inc(q_mm, 1)
                values(-1, 1)
                if has(-2):
                    b = i - 2
                    pe.wait_ge(p1t_ok, 2 * (b + 1))
                    pe.wait_ge(cn_in, 16 * (b + 1))
                    dst = bank(0, "cx")
                    for t in range(KT):
                        for c in range(SC):
                            k = P if c < 2 else LAST
                            mm = nc.tensor.matmul(dst[:, L * t:L * (t + 1)], ctx_n[0:k, c, P * t:P * (t + 1)],
                                                  p1_t[0:k, c, :], start=(c == 0), stop=(c == SC - 1))
                    mm.then_inc(cx_mm, 1)
                scores(1)
                if has(1):
                    b = i + 1
                    pe.wait_ge(ch_ok, b + 1)
                    pe.wait_ge(cl_ok, b + 1)
                    dst = bank(1, "k")
                    for k in range(KT):
                        cs = slice(SP2 * k, SP2 * (k + 1))
                        mm = product(dst[:, 0:SP2], wk_h[:, k, :], wk_l[:, k, :], c_h[:, cs], c_l[:, cs], k, KT - 1)
                    mm.then_inc(k_mm, 1)
                if has(-2):
                    b = i - 2
                    pe.wait_ge(cxt_ok, b + 1)
                    dst = bank(0, "d")
                    for k in range(KT):
                        mm = nc.tensor.matmul(dst[0:L, :], turned[:, L * k:L * (k + 1)], n_w[:, k, :],
                                              start=(k == 0), stop=(k == KT - 1))
                    mm.then_inc(d_mm, 1)
                if has(1):
                    pe.wait_ge(q_nat, i + 2)
                    turn4(1, "qt", lambda j: q_n[:, P * j:P * (j + 1)], q_tr)
                scores(2)
                turn_maxima(0, 1, 0, "c1")
                if has(1):
                    b = i + 1
                    dst = bank(1, "v")
                    for k in range(KT):
                        cs = slice(SP2 * k, SP2 * (k + 1))
                        mm = product(dst[:, 0:SP2], wv_h[:, k, :], wv_l[:, k, :], c_h[:, cs], c_l[:, cs], k, KT - 1)
                    mm.then_inc(v_mm, 1)
                    pe.wait_ge(vT_ok, b + 1)
                    dst = bank(0, "vt")
                    for c in range(SC):
                        k = P if c < 2 else LAST
                        mm = nc.tensor.matmul(dst[0:k, P * c:P * (c + 1)], vT[:, P * c:P * c + k], ident[:, :],
                                              is_transpose=True, start=True, stop=True)
                    mm.then_inc(v_tr, 1)
                scores(3)
                heads(0, 4)
                scores(4)
                if has(-1):
                    b = i - 1
                    pe.wait_ge(on_ok, b + 1)
                    dst = bank(1, "y")
                    for j in range(J):
                        mm = nc.tensor.matmul(dst[0:L, :], o_n[:, L * j:L * (j + 1)], wo_w[:, j, :],
                                              start=(j == 0), stop=(j == J - 1))
                    mm.then_inc(y_mm, 1)
                heads(4, 7)
                values(0, 0)
                heads(7, 10)
                scores(5)
                if has(-1):
                    pe.wait_ge(x1_ok, i)
                    turn4(0, "x1t", lambda j: x1[odd][:, P * j:P * (j + 1)], x1_tr)
                heads(10, 13)
                if has(-1):
                    b = i - 1
                    pe.wait_ge(x1h_ok, b + 1)
                    pe.wait_ge(x1l_ok, b + 1)
                    dst = bank(1, "xm")
                    for k in range(KT):
                        xs = slice(L * k, L * (k + 1))
                        mm = product(dst[0:L, :], x_h[:, xs], x_l[:, xs], m_h[:, k, :], m_l[:, k, :], k, KT - 1)
                    mm.then_inc(xm_mm, 1)
                heads(13, 17)
                scores(6)
                if has(-1):
                    pe.wait_ge(xm_ok, i)
                    turn4(0, "xmt", lambda j: xm_n[:, P * j:P * (j + 1)], xm_tr)
                heads(17, 21)
                turn_maxima(1, 0, 1, "c0")
                heads(21, 25)
                scores(7)
                if has(-1):
                    b = i - 1
                    pe.wait_ge(xmt_ok, b + 1)
                    pe.wait_ge(c4_in, 16 * (b + 1))
                    dst = bank(0, "s1")
                    for k in range(KT):
                        mm = nc.tensor.matmul(dst[0:L, 0:SP2], turned[:, L * k:L * (k + 1)],
                                              cT[:, SP2 * k:SP2 * (k + 1)], start=(k == 0), stop=(k == KT - 1))
                    mm.then_inc(s1_mm, 1)
                heads(25, 32)

            run_steps(nc, pe, step)

        @block.vector
        def _(dve):
            st = pr[:, :, :, :].rearrange("p a b c -> p (a b c)")
            V = nc.vector
            dve.wait_ge(prep_act, 1)
            V.tensor_tensor(wq_l[:, :, :].rearrange("p a b -> p (a b)"), st[:, 0:2048],
                            wq_h[:, :, :].rearrange("p a b -> p (a b)").bitcast(F32), ALU.subtract).then_inc(prep_dve, 1)
            dve.wait_ge(prep_act, 2)
            V.tensor_tensor(wk_l[:, :, :].rearrange("p a b -> p (a b)"), st[:, 2048:2560],
                            wk_h[:, :, :].rearrange("p a b -> p (a b)").bitcast(F32), ALU.subtract).then_inc(prep_dve, 1)
            dve.wait_ge(prep_act, 3)
            V.tensor_tensor(wv_l[:, :, :].rearrange("p a b -> p (a b)"), st[:, 2560:3072],
                            wv_h[:, :, :].rearrange("p a b -> p (a b)").bitcast(F32), ALU.subtract).then_inc(prep_dve, 1)
            dve.wait_ge(w_in[1], 128)
            dve.wait_ge(prep_pool, 1)
            V.tensor_scalar(bv_b[:, :], ones[:, :], bv_c[:, 0:1], None, ALU.mult).then_inc(prep_dve, 1)
            V.memset(half_c[:, :], -0.5).then_inc(prep_dve, 1)
            for t in range(KT):
                dve.wait_ge(prep_act, 3 + t + 1)
                src = sc_ps[:, t, :] if t < SC else mx_ps[:, 0, :]
                V.scalar_tensor_tensor(m_l[:, t, :], src, float(H) ** -0.5, m_h[:, t, :].bitcast(F32),
                                       ALU.mult, ALU.subtract).then_inc(prep_dve, 1)
            dve.wait_ge(prep_pe, 1)
            V.tensor_copy(bo_b[:, :], o_ps[0:L, :]).then_inc(prep_dve, 1)

            def step(i, par, has):
                odd = 1 - par

                def add_mask(g):
                    if not has(0):
                        return
                    b = i
                    if g == 0:
                        dve.wait_ge(mt_in[par], ring(b, par))
                    if g == 0:
                        wait(dve, pv_mm, 2 * b)
                    if g == 4:
                        dve.wait_ge(pv_mm, 2 * b + 1)
                    for c in range(2):
                        dve.wait_ge(sc_mm, 24 * b + 3 * g + c + 1)
                        V.tensor_tensor(pr[:, g % 4, c, :].rearrange("p (j l) -> p j l", j=J),
                                        sc_ps[:, c, 0:JL].rearrange("p (j l) -> p j l", j=J),
                                        mask_t[par][:, c, :].unsqueeze(1).to_broadcast([P, J, L]),
                                        ALU.add).then_inc(sc_add, 1)

                def maxima(n0, n1):
                    if not has(1):
                        return
                    b = i + 1
                    if n0 == 0:
                        dve.wait_ge(mn_in, 16 * (b + 1))
                        wait(dve, m_tr, 2 * (b - 1))
                    for n in range(n0, n1):
                        hold(dve, a_mm, NH * b + n + 1)
                        src = mx_ps[0:L, n % 2, 0:S]
                        V.tensor_tensor_reduce(out=src, in0=src, in1=mask_n[:, :], scale=1.0, scalar=-3.0e38,
                                               op0=ALU.add, op1=ALU.max,
                                               accum_out=mx[odd][:, n:n + 1]).then_inc(a_mx, 1)

                def maxima_low(b, half, w):
                    dve.wait_ge(mh_ok, 2 * b + half + 1)
                    wait(dve, m_in[half], 32 * b)
                    V.scalar_tensor_tensor(mt_l[half][:, :], work[0:16, w, 0:L], -1.0, mt_h[half][:, :].bitcast(F32),
                                           ALU.mult, ALU.subtract).then_inc(ml_ok, 1)

                if has(1):
                    b = i + 1
                    dve.wait_ge(xh_ok, b + 1)
                    wait(dve, q_mm, b)
                    wait(dve, xm_mm, i - 1)
                    V.tensor_tensor(x_l[:, :], xT[odd][:, :], x_h[:, :].bitcast(F32), ALU.subtract).then_inc(xl_ok, 1)
                    dve.wait_ge(q_mm, b + 1)
                    wait(dve, q_tr, b)
                    V.tensor_tensor(q_n[:, :], work[0:L, 1, :], bq_b[:, :], ALU.add).then_inc(q_nat, 1)
                add_mask(0)
                if has(1):
                    b = i + 1
                    dve.wait_ge(kh_ok, b + 1)
                    wait(dve, k_out, 32 * b)
                    V.scalar_tensor_tensor(k_l[:, :], work[:, 1, 0:SP2], bk_c[:, 0:1], k_h[:, :].bitcast(F32),
                                           ALU.add, ALU.subtract).then_inc(kl_ok, 1)
                add_mask(1)
                if has(-2):
                    b = i - 2
                    dve.wait_ge(d_mm, b + 1)
                    dve.wait_ge(ra_ok, b + 1)
                    V.scalar_tensor_tensor(x1[par][:, :], work[0:L, 0, :], ra[:, 0:1], x1[par][:, :],
                                           ALU.mult, ALU.add).then_inc(res_ok, 1)
                if has(1):
                    b = i + 1
                    dve.wait_ge(qh_ok, b + 1)
                    wait(dve, q_out, 32 * b)
                    V.scalar_tensor_tensor(q_l[:, :], work[:, 1, 0:JL], 0.25, q_h[:, :].bitcast(F32),
                                           ALU.mult, ALU.subtract).then_inc(ql_ok, 1)
                if has(0):
                    maxima_low(i, 1, 0)
                add_mask(2)
                add_mask(3)
                if has(-1):
                    b = i - 1
                    dve.wait_ge(ot_in, 32 * (b + 1))
                    wait(dve, rd_out, 16 * b)
                    V.reciprocal(rden[:, :], den[:, :]).then_inc(rd_ok, 1)
                maxima(0, 4)
                if has(-1):
                    b = i - 1
                    dve.wait_ge(rb_in, 16 * (b + 1))
                    V.tensor_tensor(o_n[:, :], o_n[:, :], r_b[:, :], ALU.mult).then_inc(on_ok, 1)
                maxima(4, 7)
                if has(-1):
                    b = i - 1
                    dve.wait_ge(y_mm, b + 1)
                    dve.wait_ge(xb_ok, b + 1)
                    V.tensor_tensor(y[:, :], work[0:L, 1, :], y[:, :], ALU.add).then_inc(y_ok, 1)
                    dve.wait_ge(y_ok, b + 1)
                    V.bn_stats(stats[:, :], y[:, :]).then_inc(st_ok, 1)
                    dve.wait_ge(st_ok, b + 1)
                    hold(dve, ve_ok, b)
                    V.bn_aggr(mv[:, :], stats[:, :]).then_inc(mv_ok, 1)
                add_mask(4)
                maxima(7, 10)
                if has(-1):
                    b = i - 1
                    dve.wait_ge(rstd_ok, b + 1)
                    dve.wait_ge(mv_ok, b + 1)
                    V.tensor_scalar(y[:, :], y[:, :], mv[:, 0:1], rstd[:, 0:1], ALU.subtract, ALU.mult).then_inc(xc_ok, 1)
                maxima(10, 13)
                add_mask(5)
                if has(-1):
                    b = i - 1
                    dve.wait_ge(x1h_ok, b + 1)
                    wait(dve, xm_mm, b)
                    dve.wait_ge(q_mm, upto(i + 2))
                    V.tensor_tensor(x_l[:, :], work[:, 0, 0:JL], x_h[:, :].bitcast(F32), ALU.subtract).then_inc(x1l_ok, 1)
                maxima(13, 21)
                add_mask(6)
                if has(1):
                    maxima_low(i + 1, 0, 1)
                maxima(21, 25)
                if has(-1):
                    b = i - 1
                    dve.wait_ge(s1_mm, b + 1)
                    wait(dve, p1_ok, b)
                    V.tensor_reduce(nm1[:, :], work[0:L, 0, 0:S], AX.X, ALU.max, negate=True).then_inc(nm_ok, 1)
                add_mask(7)
                maxima(25, 32)
                if has(-1):
                    b = i - 1
                    dve.wait_ge(p1_ok, b + 1)
                    wait(dve, ra_ok, b)
                    V.reciprocal(ra0[:, :], s1[:, :]).then_inc(ra0_ok, 1)
                    dve.wait_ge(ra0_ok, b + 1)
                    wait(dve, res_ok, b)
                    V.tensor_scalar(ra[:, :], ra0[:, :], alpha_c[:, 0:1], None, ALU.mult).then_inc(ra_ok, 1)

            run_steps(nc, dve, step)

        @block.scalar
        def _(act):
            st = pr[:, :, :, :].rearrange("p a b c -> p (a b c)")
            A = nc.scalar
            act.wait_ge(w_in[0], 48)
            A.activation(wq_h[:, :, :].rearrange("p a b -> p (a b)"), st[:, 0:2048], ACT.Copy).then_inc(prep_act, 1)
            A.activation(wk_h[:, :, :].rearrange("p a b -> p (a b)"), st[:, 2048:2560], ACT.Copy).then_inc(prep_act, 1)
            A.activation(wv_h[:, :, :].rearrange("p a b -> p (a b)"), st[:, 2560:3072], ACT.Copy).then_inc(prep_act, 1)
            for t in range(KT):
                act.wait_ge(prep_pe, 1 + t + 1)
                src = sc_ps[:, t, :] if t < SC else mx_ps[:, 0, :]
                A.activation(m_h[:, t, :], src, ACT.Copy, scale=float(H) ** -0.5).then_inc(prep_act, 1)
            for t in range(KT):
                act.wait_ge(prep_pe, 5 + t + 1)
                src = sc_ps[:, t, :] if t < SC else mx_ps[:, 0, :]
                A.activation(n_w[:, t, :], src, ACT.Copy).then_inc(prep_act, 1)
            act.wait_ge(prep_act, 11)

            def step(i, par, has):
                odd = 1 - par

                def copy_scores(g):
                    if not has(0):
                        return
                    b = i
                    act.wait_ge(sc_mm, 24 * b + 3 * g + 3)
                    if g == 0:
                        wait(act, pv_mm, 2 * b)
                    if g == 4:
                        act.wait_ge(pv_mm, 2 * b + 1)
                    A.activation(pr[:, g % 4, 2, :], sc_ps[:, 2, 0:JL], ACT.Copy).then_inc(sc_cp, 1)

                def probabilities(g):
                    if not has(0):
                        return
                    b = i
                    act.wait_ge(sc_add, 2 * (8 * b + g + 1))
                    act.wait_ge(sc_pool, 8 * b + g + 1)
                    t = pr[:, g % 4, :, :].rearrange("p c n -> p (c n)")
                    A.activation(t, t, ACT.Exp).then_inc(ex_ok, 1)

                def output(off, half):
                    if not has(off):
                        return
                    b = i + off
                    act.wait_ge(pv_mm, 2 * b + half + 1)
                    wait(act, os_out[half], 16 * b)
                    A.activation(o_s[half][:, :], o_ps[:, 0:JL], ACT.Copy).then_inc(os_ok, 1)

                def maxima_high(b, half, w):
                    act.wait_ge(m_tr, 2 * b + half + 1)
                    wait(act, m_in[half], 32 * b)
                    A.activation(mt_h[half][:, :], work[0:16, w, 0:L], ACT.Copy, scale=-1.0).then_inc(mh_ok, 1)

                if has(1):
                    b = i + 1
                    act.wait_ge(x_in[odd], ring(b, odd))
                    wait(act, q_mm, b)
                    wait(act, xl_ok, b)
                    wait(act, xm_mm, i - 1)
                    wait(act, x1l_ok, i - 1)
                    A.activation(x_h[:, :], xT[odd][:, :], ACT.Copy).then_inc(xh_ok, 1)
                    act.wait_ge(c_in, 16 * (b + 1))
                    wait(act, v_mm, b)
                    wait(act, cl_ok, b)
                    A.activation(c_h[:, :], cT[:, :], ACT.Copy).then_inc(ch_ok, 1)
                if has(-2):
                    b = i - 2
                    act.wait_ge(p1_tr, b + 1)
                    wait(act, cx_mm, b)
                    A.activation(p1_t[:, 0:2, :].rearrange("p c l -> p (c l)"), work[:, 0, 0:2 * L], ACT.Copy).then_inc(p1t_ok, 1)
                    A.activation(p1_t[0:LAST, 2, :], work[0:LAST, 0, 2 * L:3 * L], ACT.Copy).then_inc(p1t_ok, 1)
                output(-1, 1)
                copy_scores(0)
                if has(-2):
                    b = i - 2
                    act.wait_ge(cx_mm, b + 1)
                    wait(act, d_mm, b)
                    act.wait_ge(s1_mm, b + 1)
                    A.activation(turned[:, :], work[:, 0, 0:JL], ACT.Copy).then_inc(cxt_ok, 1)
                if has(1):
                    b = i + 1
                    act.wait_ge(k_mm, b + 1)
                    wait(act, k_out, 32 * b)
                    wait(act, kl_ok, b)
                    A.activation(k_h[:, :], work[:, 1, 0:SP2], ACT.Identity, bias=bk_c[:, 0:1]).then_inc(kh_ok, 1)
                probabilities(0)
                copy_scores(1)
                if has(1):
                    b = i + 1
                    act.wait_ge(q_tr, b + 1)
                    wait(act, q_out, 32 * b)
                    wait(act, ql_ok, b)
                    A.activation(q_h[:, :], work[:, 1, 0:JL], ACT.Copy, scale=0.25).then_inc(qh_ok, 1)
                probabilities(1)
                if has(0):
                    maxima_high(i, 1, 0)
                copy_scores(2)
                if has(1):
                    b = i + 1
                    act.wait_ge(v_mm, b + 1)
                    wait(act, v_tr, b)
                    A.activation(vT[:, :], work[:, 1, 0:SP2], ACT.Copy).then_inc(vT_ok, 1)
                probabilities(2)
                copy_scores(3)
                if has(1):
                    b = i + 1
                    act.wait_ge(v_tr, b + 1)
                    wait(act, pv_mm, 2 * (b - 1))
                    for c0, c1, k in ((0, 2, P), (2, 3, LAST)):
                        A.activation(va[odd][0:k, c0:c1, :, 0:HD].rearrange("p c g d -> p (c g) d"),
                                     work[0:k, 0, P * c0:P * c1].rearrange("p (n d) -> p n d", d=HD),
                                     ACT.Copy).then_inc(va_ok, 1)
                probabilities(3)
                copy_scores(4)
                output(0, 0)
                probabilities(4)
                if has(-1):
                    b = i - 1
                    act.wait_ge(x1_tr, b + 1)
                    act.wait_ge(q_mm, upto(i + 2))
                    act.wait_ge(xl_ok, upto(i + 2))
                    wait(act, xm_mm, b)
                    A.activation(x_h[:, :], work[:, 0, 0:JL], ACT.Copy).then_inc(x1h_ok, 1)
                copy_scores(5)
                if has(-1):
                    b = i - 1
                    act.wait_ge(xm_mm, b + 1)
                    wait(act, xm_tr, b)
                    A.activation(xm_n[:, :], work[0:L, 1, :], ACT.Copy).then_inc(xm_ok, 1)
                probabilities(5)
                if has(-1):
                    b = i - 1
                    act.wait_ge(xm_tr, b + 1)
                    wait(act, s1_mm, b)
                    wait(act, d_mm, b)
                    A.activation(turned[:, :], work[:, 0, 0:JL], ACT.Copy).then_inc(xmt_ok, 1)
                copy_scores(6)
                if has(1):
                    maxima_high(i + 1, 0, 1)
                probabilities(6)
                copy_scores(7)
                if has(-1):
                    b = i - 1
                    act.wait_ge(nm_ok, b + 1)
                    wait(act, p1_tr, b)
                    wait(act, ra0_ok, b)
                    A.activation(p1[:, 0:S], work[0:L, 0, 0:S], ACT.Exp, bias=nm1[:, 0:1],
                                 accum_out=s1[:, :]).then_inc(p1_ok, 1)
                probabilities(7)

            run_steps(nc, act, step)

        @block.gpsimd
        def _(pool):
            G = nc.gpsimd
            pool.memset(ones[:, :], 1.0).then_inc(prep_pool, 1)
            pool.memset(ident[:, :], 0.0).then_inc(prep_pool, 1)
            pool.wait_ge(prep_pool, 2)
            pool.affine_select(out=ident[:, :], in_=ident[:, :], compare_op=ALU.not_equal, fill=1.0, base=0,
                               pattern=[[-1, P]], channel_multiplier=1).then_inc(prep_pool, 1)
            for p in range(2):
                pool.wait_ge(prep_pool, 3 + 3 * p)
                pool.memset(ks[p][0:64, :, SP2:SC * P].bitcast(F32), 0.0).then_inc(prep_pool, 1)
                pool.wait_ge(prep_pool, 4 + 3 * p)
                pool.memset(va[p][:, :, :, HD:2 * HD], 1.0).then_inc(prep_pool, 1)
                pool.wait_ge(prep_pool, 5 + 3 * p)
                pool.memset(ks[p][64:66, :, 0:SC * P].bitcast(F32), 1.0).then_inc(prep_pool, 1)
            pool.wait_ge(prep_pool, 9)

            def step(i, par, has):
                odd = 1 - par

                def add_mask(g):
                    if not has(0):
                        return
                    b = i
                    if g == 0:
                        pool.wait_ge(mt_in[par], ring(b, par))
                    pool.wait_ge(sc_cp, 8 * b + g + 1)
                    t = pr[:, g % 4, 2, :].rearrange("p (j l) -> p j l", j=J)
                    G.tensor_tensor(t, t, mask_t[par][:, 2, :].unsqueeze(1).to_broadcast([P, J, L]),
                                    ALU.add).then_inc(sc_pool, 1)

                if has(1):
                    b = i + 1
                    pool.wait_ge(ch_ok, b + 1)
                    wait(pool, v_mm, b)
                    G.tensor_tensor(c_l[:, :], cT[:, :], c_h[:, :].bitcast(F32), ALU.subtract).then_inc(cl_ok, 1)
                add_mask(0)
                add_mask(1)
                if has(-1):
                    b = i - 1
                    pool.wait_ge(xn_in, 16 * (b + 1))
                    pool.wait_ge(prep_dve, 10)
                    G.tensor_tensor(y[:, :], y[:, :], bo_b[:, :], ALU.add).then_inc(xb_ok, 1)
                add_mask(2)
                add_mask(3)
                if has(-1):
                    b = i - 1
                    pool.wait_ge(mv_ok, b + 1)
                    hold(pool, rstd_ok, b)
                    G.tensor_scalar(ve[:, :], mv[:, 1:2], EPS, None, ALU.add).then_inc(ve_ok, 1)
                    pool.wait_ge(ve_ok, b + 1)
                    wait(pool, xc_ok, b)
                    G.tensor_tensor(rstd[:, :], ve[:, :], half_c[:, :], ALU.pow).then_inc(rstd_ok, 1)
                    pool.wait_ge(xc_ok, b + 1)
                    if not isinstance(b, int) or b >= 2:
                        pool.wait_ge(out_ok[odd], ring(b - 2, odd))
                    G.tensor_tensor(x1[odd][:, :], y[:, :], gamma_b[:, :], ALU.mult).then_inc(xg_ok, 1)
                    pool.wait_ge(xg_ok, b + 1)
                    G.tensor_tensor(x1[odd][:, :], x1[odd][:, :], beta_b[:, :], ALU.add).then_inc(x1_ok, 1)
                for g in range(4, KVH):
                    add_mask(g)

            run_steps(nc, pool, step)


_INS = ("xT", "x", "ctxT", "ctx", "mask", "maskT", "wq", "wk", "wv", "wo", "bq", "bk", "bv", "bo",
        "gamma", "beta", "w1q", "w1k", "w1v", "w1o", "alpha")


def kernel(**inputs):
    import numpy as np
    import concourse.bacc as bacc
    from concourse.bass_utils import run_bass_kernel_spmd as run

    a = {k: np.asarray(v) for k, v in inputs.items()}

    def rows(w):
        return w.reshape(KT, P, -1).transpose(1, 0, 2).reshape(P, -1)

    def by_head(w):
        return w.reshape(-1, KVH, J, HD).transpose(0, 2, 1, 3).reshape(-1, H)

    def chunks(t, size, pieces):
        t = np.pad(t, ((0, 0), (0, size * pieces - t.shape[1]), (0, 0)))
        return t.reshape(B, pieces, size, -1).transpose(0, 2, 1, 3)

    x, c, mask = a["x"], a["ctx_2048"], a["mask_Bx1xSxS2_ff0"][:, 0]
    cT = np.pad(c.transpose(0, 2, 1), ((0, 0), (0, 0), (0, SP2 - S)))
    arrays = {
        "xT": chunks(x.transpose(0, 2, 1), P, KT).reshape(B, P, -1),
        "x": x,
        "ctxT": chunks(cT, P, KT).reshape(B, P, -1),
        "ctx": chunks(c, P, SC),
        "mask": mask,
        "maskT": chunks(mask.transpose(0, 2, 1), P, SC),
        "wq": rows(by_head(a["L0_xattn_Wq"])),
        "wk": rows(a["L0_xattn_Wk"]),
        "wv": rows(a["L0_xattn_Wv"]),
        "wo": rows(a["L0_xattn_Wo"].reshape(KVH, J, HD, H).transpose(1, 0, 2, 3).reshape(H, H)),
        "bq": np.broadcast_to(by_head(a["L0_xattn_bq"].reshape(1, H)), (L, H)),
        "bk": a["L0_xattn_bk"].reshape(P, 1),
        "bv": a["L0_xattn_bv"].reshape(P, 1),
        "bo": a["L0_xattn_bo"].reshape(1, H),
        "gamma": np.broadcast_to(a["L0_xattn_gamma"], (L, H)),
        "beta": np.broadcast_to(a["L0_xattn_beta"], (L, H)),
        "w1q": rows(a["L1_xattn_w_q"]),
        "w1k": rows(a["L1_xattn_w_k"]),
        "w1v": rows(a["L1_xattn_w_v"]),
        "w1o": rows(a["L1_xattn_w_o"].T),
        "alpha": np.broadcast_to(a["L1_xattn_alpha"].reshape(1, 1), (L, 1)),
    }
    nc = bacc.Bacc("TRN2", target_bir_lowering=False, num_devices=1)
    feeds, args = {}, []
    for name in _INS:
        t = np.ascontiguousarray(arrays[name])
        feeds[f"in_{name}"] = t
        args.append(nc.dram_tensor(f"in_{name}", t.shape, mybir.dt.from_np(t.dtype), kind="ExternalInput").ap())
    args.append(nc.dram_tensor("out", (B, L, H), F32, kind="ExternalOutput").ap())
    build(nc, *args)
    return run(nc, [feeds], core_ids=[0]).results[0]["out"]
```

```python
from contextlib import ExitStack

import concourse.bass as bass
from concourse import mybir

F32 = mybir.dt.float32
F32R = mybir.dt.float32r
ACT = mybir.ActivationFunctionType
ALU = mybir.AluOpType
AX = mybir.AxisListType

B, L, S, H = 16, 100, 361, 512
NH, KVH, HD = 32, 8, 16
J = NH // KVH
P = 128
KT = H // P
SP2 = S + 1
SC = 3
LAST = S - 2 * P
JL = J * L
EPS = 1e-6

LOOP = (2, 14)
STEPS = (-2, B + 2)

BANK_USERS = (
    (("p1t", -2, "p1t_ok", 2, 2), ("cx", -2, "cxt_ok", 1, 1), ("d", -2, "res_ok", 1, 1), ("y", -1, "y_ok", 1, 1),
     ("x1t", -1, "x1l_ok", 1, 1), ("xm", -1, "xm_ok", 1, 1), ("xmt", -1, "xmt_ok", 1, 1), ("s1", -1, "p1_ok", 1, 1)),
    (("c1", 0, "ml_ok", 2, 2), ("vt", 1, "va_ok", 2, 2), ("q", 2, "q_nat", 1, 1), ("qt", 2, "ql_ok", 1, 1),
     ("k", 2, "kl_ok", 1, 1), ("c0", 1, "ml_ok", 2, 1), ("v", 2, "vT_ok", 1, 1)),
)


def in_range(batch):
    return 0 <= batch < B


def upto(count):
    return min(count, B) if isinstance(count, int) else count


def emptied(bank, piece, i):
    users = BANK_USERS[bank]
    at = [user[0] for user in users].index(piece)
    for back in range(1, 3 * len(users)):
        behind, before = divmod(at - back, len(users))
        _, off, name, each, done = users[before]
        batch = i + behind + off
        if not isinstance(i, int) or in_range(batch):
            return name, each * batch + done
    return None, 0


def wait(eng, sem, value):
    if not (isinstance(value, int) and value <= 0):
        eng.wait_ge(sem, value)


def hold(eng, sem, value):
    wait(eng, sem, value)
    if not isinstance(value, int):
        eng.nop(nofuse=True)


def ring(b, par, dmas=1):
    return (8 * b - 8 * par + 16) * dmas


def run_steps(nc, eng, body, after=None):
    for i in range(STEPS[0], LOOP[0]):
        body(i, i % 2, lambda off, i=i: in_range(i + off))
        if after and i < 0:
            after(i)
    with eng.Fori(LOOP[0], LOOP[1], 2) as i:
        i = nc.s_assert_within(i, LOOP[0], LOOP[1] - 2,
                               skip_runtime_bounds_check_because="the loop goes by two and its range is even")
        body(i, 0, lambda off: True)
        body(i + 1, 1, lambda off: True)
    for i in range(LOOP[1], STEPS[1]):
        body(i, i % 2, lambda off, i=i: in_range(i + off))


def build(nc, xT_d, x_d, ctxT_d, ctx_d, mask_d, maskT_d, wq_d, wk_d, wv_d, wo_d, bq_d, bk_d, bv_d,
          bo_d, gamma_d, beta_d, w1q_d, w1k_d, w1v_d, w1o_d, alpha_d, out_d):
    with ExitStack() as ctx:
        def sb(name, shape, dt=F32):
            return ctx.enter_context(nc.sbuf_tensor(name, shape, dt))

        def sem(name):
            return ctx.enter_context(nc.semaphore(name))

        sc_ps = ctx.enter_context(nc.psum_tensor("sc_ps", [P, SC, 512], F32))
        mx_ps = ctx.enter_context(nc.psum_tensor("mx_ps", [P, 2, 512], F32))
        o_ps = ctx.enter_context(nc.psum_tensor("o_ps", [P, 512], F32))
        work = ctx.enter_context(nc.psum_tensor("work", [P, 2, 512], F32))

        wq_h, wq_l = sb("wq_h", [P, KT, H], F32R), sb("wq_l", [P, KT, H], F32R)
        wk_h, wk_l = sb("wk_h", [P, KT, P], F32R), sb("wk_l", [P, KT, P], F32R)
        wv_h, wv_l = sb("wv_h", [P, KT, P], F32R), sb("wv_l", [P, KT, P], F32R)
        m_h, m_l = sb("m_h", [P, KT, H], F32R), sb("m_l", [P, KT, H], F32R)
        n_w = sb("n_w", [P, KT, H])
        wo_w = sb("wo_w", [P, J, H])
        bq_b, gamma_b, beta_b, bo_b = (sb(n, [L, H]) for n in ("bq_b", "gamma_b", "beta_b", "bo_b"))
        bk_c, bv_c = sb("bk_c", [P, 1]), sb("bv_c", [P, 1])
        bo_r = sb("bo_r", [1, H])
        alpha_c = sb("alpha_c", [L, 1])
        half_c = sb("half_c", [L, 1])
        ident = sb("ident", [P, P])
        ones = sb("ones", [P, L])
        bv_b = sb("bv_b", [P, L])

        xT = sb("xT", [P, KT * L])
        cT = sb("cT", [P, KT * SP2])
        x_h, x_l = sb("x_h", [P, JL], F32R), sb("x_l", [P, JL], F32R)
        c_h, c_l = sb("c_h", [P, KT * SP2], F32R), sb("c_l", [P, KT * SP2], F32R)
        q_n = sb("q_n", [L, H])
        q_h, q_l = sb("q_h", [P, JL], F32R), sb("q_l", [P, JL], F32R)
        k_h, k_l = sb("k_h", [P, SP2], F32R), sb("k_l", [P, SP2], F32R)
        vT = sb("vT", [P, SP2])
        va = [sb(f"va{p}", [P, SC, KVH, 2 * HD]) for p in range(2)]
        qs = [sb(f"qs{p}", [66, KVH, JL], F32R) for p in range(2)]
        ks = [sb(f"ks{p}", [66, KVH, SC * P], F32R) for p in range(2)]
        mask_n = [sb(f"mask_n{p}", [L, S]) for p in range(2)]
        mx = [sb(f"mx{p}", [L, NH]) for p in range(2)]
        mt_h = [sb(f"mt_h{h}", [NH // 2, L], F32R) for h in range(2)]
        mt_l = [sb(f"mt_l{h}", [NH // 2, L], F32R) for h in range(2)]

        mask_t = [sb(f"mask_t{p}", [P, SC, L]) for p in range(2)]
        pr = sb("pr", [P, 4, SC, JL])
        o_s = [sb(f"o_s{h}", [P, JL]) for h in range(2)]

        o_n, r_b = sb("o_n", [P, JL]), sb("r_b", [P, JL])
        y = sb("y", [L, H])
        stats, mv, ve, rstd = sb("stats", [L, 6]), sb("mv", [L, 2]), sb("ve", [L, 1]), sb("rstd", [L, 1])
        x1 = [sb(f"x1_{p}", [L, H]) for p in range(2)]
        xm_n = sb("xm_n", [L, H])
        nm1, s1, ra0, ra = sb("nm1", [L, 1]), sb("s1", [L, 1]), sb("ra0", [L, 1]), sb("ra", [L, 1])
        p1, p1_t = sb("p1", [L, SP2]), sb("p1_t", [P, SC, L])
        ctx_n = sb("ctx_n", [P, SC, H])
        turned = sb("turned", [P, JL])

        k_dr = nc.dram_tensor("k_dr", (2, 2, P, SP2), F32, kind="Internal").ap()
        q_dr = nc.dram_tensor("q_dr", (2, 2, P, JL), F32, kind="Internal").ap()
        o_dr = nc.dram_tensor("o_dr", (2, KVH * 32, JL), F32, kind="Internal").ap()

        w_in = [sem(f"w_in{n}") for n in range(5)]
        prep_act, prep_dve, prep_pool, prep_pe = sem("prep_act"), sem("prep_dve"), sem("prep_pool"), sem("prep_pe")
        x_in = sem("x_in")
        c_in = sem("c_in")
        c4_in = sem("c4_in")
        xh_ok, xl_ok, ch_ok, cl_ok = (sem(n) for n in ("xh_ok", "xl_ok", "ch_ok", "cl_ok"))
        q_mm, q_nat, q_tr, qh_ok, ql_ok = (sem(n) for n in ("q_mm", "q_nat", "q_tr", "qh_ok", "ql_ok"))
        k_mm, kh_ok, kl_ok = sem("k_mm"), sem("kh_ok"), sem("kl_ok")
        v_mm, vT_ok, v_tr, va_ok = sem("v_mm"), sem("vT_ok"), sem("v_tr"), sem("va_ok")
        k_out, q_out = sem("k_out"), sem("q_out")
        st_in = [sem(f"st_in{h}") for h in range(2)]
        mn_in = [sem(f"mn_in{p}") for p in range(2)]
        mt_in = [sem(f"mt_in{p}") for p in range(2)]
        a_mm, a_mx = sem("a_mm"), sem("a_mx")
        m_tr, mh_ok, ml_ok = sem("m_tr"), sem("mh_ok"), sem("ml_ok")
        m_in = [sem(f"m_in{h}") for h in range(2)]
        sc_mm = sem("sc_mm")
        sc_add, sc_cp, sc_pool = sem("sc_add"), sem("sc_cp"), sem("sc_pool")
        ex_ok = sem("ex_ok")
        pv_mm, os_ok = sem("pv_mm"), sem("os_ok")
        os_out = [sem(f"os_out{h}") for h in range(2)]
        ot_in, r_ok, on_ok = sem("ot_in"), sem("r_ok"), sem("on_ok")
        xn_in, xb_ok = sem("xn_in"), sem("xb_ok")
        y_mm, y_ok, st_ok, mv_ok, ve_ok, rstd_ok, xc_ok, xg_ok, x1_ok = (
            sem(n) for n in ("y_mm", "y_ok", "st_ok", "mv_ok", "ve_ok", "rstd_ok", "xc_ok", "xg_ok", "x1_ok"))
        x1_tr, x1h_ok, x1l_ok = sem("x1_tr"), sem("x1h_ok"), sem("x1l_ok")
        xm_mm, xm_ok, xm_tr, xmt_ok = sem("xm_mm"), sem("xm_ok"), sem("xm_tr"), sem("xmt_ok")
        s1_mm, nm_ok, p1_ok, ra0_ok, ra_ok = (sem(n) for n in ("s1_mm", "nm_ok", "p1_ok", "ra0_ok", "ra_ok"))
        p1_tr, p1t_ok, cn_in, cx_mm, cxt_ok = (sem(n) for n in ("p1_tr", "p1t_ok", "cn_in", "cx_mm", "cxt_ok"))
        d_mm, res_ok = sem("d_mm"), sem("res_ok")
        out_ok = [sem(f"out_ok{p}") for p in range(2)]

        block = ctx.enter_context(nc.Block())

        @block.sync
        def _(sp):
            st = pr[:, :, :, :].rearrange("p a b c -> p (a b c)")
            sp.dma_start(st[:, 0:2048], wq_d).then_inc(w_in[0], 16)
            sp.dma_start(st[:, 2048:2560], wk_d).then_inc(w_in[0], 16)
            sp.dma_start(st[:, 2560:3072], wv_d).then_inc(w_in[0], 16)
            sp.dma_start(wo_w[:, :, :].rearrange("p a b -> p (a b)"), wo_d).then_inc(w_in[1], 16)
            sp.dma_start(bq_b[:, :], bq_d).then_inc(w_in[1], 16)
            sp.dma_start(gamma_b[:, :], gamma_d).then_inc(w_in[1], 16)
            sp.dma_start(beta_b[:, :], beta_d).then_inc(w_in[1], 16)
            sp.dma_start(bk_c[:, :], bk_d).then_inc(w_in[1], 16)
            sp.dma_start(bv_c[:, :], bv_d).then_inc(w_in[1], 16)
            sp.dma_start(bo_r[:, :], bo_d).then_inc(w_in[1], 16)
            sp.dma_start(alpha_c[:, :], alpha_d).then_inc(w_in[1], 16)

            def after(i):
                if i == STEPS[0]:
                    sp.wait_ge(prep_pe, 5)
                    sp.dma_start(st[:, 0:2048], w1v_d).then_inc(w_in[3], 16)
                    sp.dma_start(st[:, 2048:4096], w1o_d).then_inc(w_in[3], 16)

            def step(i, par, has):
                odd = 1 - par

                def stack_in(b, p, half):
                    gs = slice(4 * half, 4 * half + 4)
                    for r in range(4):
                        sp.dma_start(ks[p][HD * r:HD * (r + 1), gs, 0:SP2].bitcast(F32),
                                     k_dr[p, r // 2, :, :].rearrange("(g d) s -> d g s", d=HD)[:, gs, :]
                                     ).then_inc(st_in[half], 16)
                        sp.dma_start(qs[p][HD * r:HD * (r + 1), gs, :].bitcast(F32),
                                     q_dr[p, r % 2, :, :].rearrange("(g d) c -> d g c", d=HD)[:, gs, :]
                                     ).then_inc(st_in[half], 16)

                def maxima_in(b, half, stack):
                    hold(sp, mh_ok, 2 * b + half + 1)
                    hold(sp, ml_ok, 2 * b + half + 1)
                    for row, t in ((64, mt_h[half]), (65, mt_l[half])):
                        dst = stack[row:row + 1, 4 * half:4 * half + 4, :].bitcast(F32).rearrange(
                            "p g (j l) -> p (g j) l", j=J)
                        sp.dma_start(dst, t[:, :].bitcast(F32)).then_inc(m_in[half], 16)

                if has(2):
                    b = i + 2
                    hold(sp, xh_ok, b)
                    hold(sp, xl_ok, b)
                    sp.dma_start(xT[:, :], xT_d[b, :, :]).then_inc(x_in, 16)
                if has(1):
                    hold(sp, sc_mm, 24 * i)
                    stack_in(i + 1, odd, 1)
                if has(2):
                    b = i + 2
                    hold(sp, ch_ok, b)
                    hold(sp, cl_ok, b)
                    hold(sp, s1_mm, i - 1)
                    sp.dma_start(cT[:, :], ctxT_d[b, :, :]).then_inc(c_in, 16)
                if has(0):
                    maxima_in(i, 1, qs[par])
                if has(2):
                    b = i + 2
                    hold(sp, a_mx, NH * (i + 1))
                    sp.dma_start(mask_n[par][:, :], mask_d[b, :, :]).then_inc(mn_in[par], 16)
                if has(-1):
                    b = i - 1
                    hold(sp, os_ok, 2 * b + 2)
                    sp.dma_start(o_dr[odd, P:2 * P, :], o_s[1][:, :]).then_inc(os_out[1], 16)
                    hold(sp, xg_ok, b)
                    sp.dma_start(y[:, :], x_d[b, :, :]).then_inc(xn_in, 16)
                    hold(sp, os_out[0], 16 * (b + 1))
                    hold(sp, os_out[1], 16 * (b + 1))
                    hold(sp, y_mm, b)
                    hold(sp, on_ok, J * b)
                    rows = o_dr[odd, :, :].rearrange("(g r) c -> g r c", r=2 * HD)
                    sp.dma_start(r_b[:, :], rows[:, HD:2 * HD, :]).then_inc(ot_in, 16)
                    sp.dma_start(o_n[:, :], rows[:, 0:HD, :]).then_inc(ot_in, 16)
                if has(1):
                    hold(sp, sc_add, 16 * i)
                    hold(sp, sc_pool, 8 * i)
                    sp.dma_start(mask_t[odd][:, :, :], maskT_d[i + 1, :, :, :]).then_inc(mt_in[odd], 16)
                if has(-1):
                    b = i - 1
                    hold(sp, ch_ok, upto(i + 3))
                    hold(sp, cl_ok, upto(i + 3))
                    hold(sp, s1_mm, b)
                    sp.dma_start(cT[:, :], ctxT_d[b, :, :]).then_inc(c4_in, 16)
                    hold(sp, cx_mm, b)
                    sp.dma_start(ctx_n[:, :, :], ctx_d[b, :, :, :]).then_inc(cn_in, 16)
                if has(-2):
                    b = i - 2
                    hold(sp, res_ok, b + 1)
                    sp.dma_start(out_d[b, :, :], x1[par][:, :]).then_inc(out_ok[par], 16)
                if has(1):
                    maxima_in(i + 1, 0, qs[odd])
                if has(0):
                    hold(sp, os_ok, 2 * i + 1)
                    hold(sp, ot_in, 32 * (i - 1))
                    sp.dma_start(o_dr[par, 0:P, :], o_s[0][:, :]).then_inc(os_out[0], 16)
                if has(2):
                    b = i + 2
                    hold(sp, qh_ok, b + 1)
                    hold(sp, ql_ok, b + 1)
                    hold(sp, st_in[1], 128 * (b - 1))
                    sp.dma_start(q_dr[par, 0, :, :], q_h[:, :].bitcast(F32)).then_inc(q_out, 16)
                    sp.dma_start(q_dr[par, 1, :, :], q_l[:, :].bitcast(F32)).then_inc(q_out, 16)
                    hold(sp, kh_ok, b + 1)
                    hold(sp, kl_ok, b + 1)
                    sp.dma_start(k_dr[par, 0, :, :], k_h[:, :].bitcast(F32)).then_inc(k_out, 16)
                    sp.dma_start(k_dr[par, 1, :, :], k_l[:, :].bitcast(F32)).then_inc(k_out, 16)
                    hold(sp, q_out, 32 * (b + 1))
                    hold(sp, k_out, 32 * (b + 1))
                    hold(sp, sc_mm, 24 * i + 12)
                    stack_in(b, par, 0)

            run_steps(nc, sp, step, after)
            for p in range(2):
                sp.wait_ge(out_ok[p], 16 * (B // 2))

        @block.tensor
        def _(pe):
            bank_read = dict(p1t_ok=p1t_ok, cxt_ok=cxt_ok, res_ok=res_ok, ml_ok=ml_ok, va_ok=va_ok, x1l_ok=x1l_ok,
                             xmt_ok=xmt_ok, p1_ok=p1_ok, q_nat=q_nat, kl_ok=kl_ok, ql_ok=ql_ok, vT_ok=vT_ok,
                             y_ok=y_ok, xm_ok=xm_ok)
            st = pr[:, :, :, :].rearrange("p a b c -> p (a b c)")
            pe.wait_ge(w_in[1], 128)
            pe.wait_ge(prep_dve, 4)
            pe.wait_ge(prep_pool, 9)
            for j in range(J):
                nc.tensor.matmul(o_ps[0:L, :], bv_b[:, :], wo_w[:, j, :], start=(j == 0), stop=False)
            nc.tensor.matmul(o_ps[0:L, :], ones[0:1, :], bo_r[:, :], start=False, stop=True).then_inc(prep_pe, 1)

            def after(i):
                n = i - STEPS[0]
                pe.wait_ge(w_in[2 + n], 32)
                for t in range(KT):
                    dst = sc_ps[:, t, :] if t < SC else o_ps[:, :]
                    if n == 0 and t == SC:
                        pe.wait_ge(prep_dve, 6)
                    if n == 1:
                        pe.wait_ge(prep_act, 3 + t + 1)
                        pe.wait_ge(prep_dve, 6 + t + 1)
                    for o in range(KT):
                        mm = nc.tensor.matmul(dst, st[:, 512 * o + P * t:512 * o + P * (t + 1)],
                                              st[:, 2048 + 512 * o:2048 + 512 * (o + 1)],
                                              start=(o == 0), stop=(o == KT - 1))
                    mm.then_inc(prep_pe, 1)
                if n == 1:
                    pe.wait_ge(prep_act, 11)

            def product(dst, lh, ll, rh, rl, k, last):
                nc.tensor.matmul(dst, lh, rh, start=(k == 0), stop=False)
                nc.tensor.matmul(dst, lh, rl, start=False, stop=False)
                return nc.tensor.matmul(dst, ll, rh, start=False, stop=(k == last))

            def step(i, par, has):
                odd = 1 - par

                def bank(w, piece):
                    name, count = emptied(w, piece, i)
                    wait(pe, bank_read.get(name), count)
                    return work[:, w, :]

                def scores(g):
                    if not has(0):
                        return
                    b = i
                    if g == 0:
                        pe.wait_ge(m_in[0], 32 * (b + 1))
                    if g == KVH // 2:
                        pe.wait_ge(m_in[1], 32 * (b + 1))
                    for c in range(SC):
                        if c < 2:
                            wait(pe, sc_add, 2 * (8 * b + g - 1) + c + 1)
                        else:
                            wait(pe, sc_cp, 8 * b + g)
                        nc.tensor.matmul(sc_ps[:, c, 0:JL], ks[par][:, g, P * c:P * (c + 1)], qs[par][:, g, :],
                                         start=True, stop=True).then_inc(sc_mm, 1)

                def heads(n0, n1):
                    if not has(1):
                        return
                    b = i + 1
                    for n in range(n0, n1):
                        g, j = n // J, n % J
                        if n % (NH // 2) == 0:
                            pe.wait_ge(st_in[n // (NH // 2)], 128 * (b + 1))
                        wait(pe, a_mx, NH * b + n - 1)
                        nc.tensor.matmul(mx_ps[0:L, n % 2, 0:SP2], qs[odd][0:64, g, L * j:L * (j + 1)],
                                         ks[odd][0:64, g, 0:SP2], start=True, stop=True).then_inc(a_mm, 1)

                def values(off, half):
                    if not has(off):
                        return
                    b, p = i + off, (par + off) % 2
                    pe.wait_ge(ex_ok, 8 * b + 4 * half + 4)
                    if half == 0:
                        pe.wait_ge(va_ok, 2 * (b + 1))
                    wait(pe, os_ok, 2 * b + half)
                    for c in range(SC):
                        k = P if c < 2 else LAST
                        for q in range(4):
                            mm = nc.tensor.matmul(o_ps[32 * q:32 * (q + 1), 0:JL], va[p][0:k, c, 4 * half + q, :],
                                                  pr[0:k, q, c, :], start=(c == 0), stop=(c == SC - 1))
                    mm.then_inc(pv_mm, 1)

                def turn_maxima(off, half, w, piece):
                    if not has(off):
                        return
                    b, p = i + off, (par + off) % 2
                    pe.wait_ge(a_mx, NH * b + 16 * (half + 1))
                    dst = bank(w, piece)
                    nc.tensor.matmul(dst[0:16, 0:L], mx[p][:, 16 * half:16 * half + 16], ident[0:L, 0:L],
                                     is_transpose=True, start=True, stop=True).then_inc(m_tr, 1)

                def turn4(w, piece, src, done):
                    dst = bank(w, piece)
                    for j in range(KT):
                        mm = nc.tensor.matmul(dst[:, L * j:L * (j + 1)], src(j), ident[0:L, 0:L],
                                              is_transpose=True, start=True, stop=True)
                    mm.then_inc(done, 1)

                def q_part(k0, k1):
                    if not has(2):
                        return
                    if k0 == 0:
                        pe.wait_ge(xh_ok, i + 3)
                        pe.wait_ge(xl_ok, i + 3)
                        bank(1, "q")
                    for k in range(k0, k1):
                        xs = slice(L * k, L * (k + 1))
                        mm = product(work[0:L, 1, :], x_h[:, xs], x_l[:, xs], wq_h[:, k, :], wq_l[:, k, :], k, KT - 1)
                    if k1 == KT:
                        mm.then_inc(q_mm, 1)

                def ctx_part(piece, w_h, w_l, k0, k1, done):
                    if not has(2):
                        return
                    if k0 == 0:
                        pe.wait_ge(ch_ok, i + 3)
                        pe.wait_ge(cl_ok, i + 3)
                        bank(1, piece)
                    for k in range(k0, k1):
                        cs = slice(SP2 * k, SP2 * (k + 1))
                        mm = product(work[:, 1, 0:SP2], w_h[:, k, :], w_l[:, k, :], c_h[:, cs], c_l[:, cs], k, KT - 1)
                    if k1 == KT:
                        mm.then_inc(done, 1)

                def cx_part(t0, t1):
                    if not has(-2):
                        return
                    if t0 == 0:
                        pe.wait_ge(p1t_ok, 2 * (i - 1))
                        pe.wait_ge(cn_in, 16 * (i - 1))
                        bank(0, "cx")
                    for t in range(t0, t1):
                        for c in range(SC):
                            k = P if c < 2 else LAST
                            mm = nc.tensor.matmul(work[:, 0, L * t:L * (t + 1)], ctx_n[0:k, c, P * t:P * (t + 1)],
                                                  p1_t[0:k, c, :], start=(c == 0), stop=(c == SC - 1))
                    if t1 == KT:
                        mm.then_inc(cx_mm, 1)

                def d_part(k0, k1):
                    if not has(-2):
                        return
                    if k0 == 0:
                        pe.wait_ge(cxt_ok, i - 1)
                        bank(0, "d")
                    for k in range(k0, k1):
                        mm = nc.tensor.matmul(work[0:L, 0, :], turned[:, L * k:L * (k + 1)], n_w[:, k, :],
                                              start=(k == 0), stop=(k == KT - 1))
                    if k1 == KT:
                        mm.then_inc(d_mm, 1)

                def y_part(j0, j1):
                    if not has(-1):
                        return
                    if j0 == 0:
                        bank(0, "y")
                    for j in range(j0, j1):
                        pe.wait_ge(on_ok, J * (i - 1) + j + 1)
                        mm = nc.tensor.matmul(work[0:L, 0, :], o_n[:, L * j:L * (j + 1)], wo_w[:, j, :],
                                              start=(j == 0), stop=(j == J - 1))
                    if j1 == J:
                        mm.then_inc(y_mm, 1)

                def xm_part(k0, k1):
                    if not has(-1):
                        return
                    if k0 == 0:
                        pe.wait_ge(x1h_ok, i)
                        pe.wait_ge(x1l_ok, i)
                        bank(0, "xm")
                    for k in range(k0, k1):
                        xs = slice(L * k, L * (k + 1))
                        mm = product(work[0:L, 0, :], x_h[:, xs], x_l[:, xs], m_h[:, k, :], m_l[:, k, :], k, KT - 1)
                    if k1 == KT:
                        mm.then_inc(xm_mm, 1)

                def s1_part(k0, k1):
                    if not has(-1):
                        return
                    if k0 == 0:
                        pe.wait_ge(xmt_ok, i)
                        pe.wait_ge(c4_in, 16 * i)
                        bank(0, "s1")
                    for k in range(k0, k1):
                        mm = nc.tensor.matmul(work[0:L, 0, 0:SP2], turned[:, L * k:L * (k + 1)],
                                              cT[:, SP2 * k:SP2 * (k + 1)], start=(k == 0), stop=(k == KT - 1))
                    if k1 == KT:
                        mm.then_inc(s1_mm, 1)

                def turn_p1():
                    if not has(-2):
                        return
                    pe.wait_ge(p1_ok, i - 1)
                    bank(0, "p1t")
                    for c in range(SC):
                        k = P if c < 2 else LAST
                        mm = nc.tensor.matmul(work[0:k, 0, L * c:L * (c + 1)], p1[:, P * c:P * c + k], ident[0:L, 0:L],
                                              is_transpose=True, start=True, stop=True)
                    mm.then_inc(p1_tr, 1)

                def turn_v():
                    if not has(1):
                        return
                    pe.wait_ge(vT_ok, i + 2)
                    bank(1, "vt")
                    for c in range(SC):
                        k = P if c < 2 else LAST
                        mm = nc.tensor.matmul(work[0:k, 1, P * c:P * (c + 1)], vT[:, P * c:P * c + k], ident[:, :],
                                              is_transpose=True, start=True, stop=True)
                    mm.then_inc(v_tr, 1)

                scores(0)
                heads(0, 2)
                turn_maxima(0, 1, 1, "c1")
                values(-1, 1)
                turn_v()
                heads(2, 4)
                turn_p1()
                q_part(0, 1)
                scores(1)
                heads(4, 5)
                q_part(1, 3)
                heads(5, 6)
                q_part(3, 4)
                heads(6, 7)
                cx_part(0, 2)
                heads(7, 8)
                cx_part(2, 3)
                scores(2)
                heads(8, 9)
                cx_part(3, 4)
                heads(9, 10)
                d_part(0, 2)
                heads(10, 11)
                if has(2):
                    pe.wait_ge(q_nat, i + 3)
                    turn4(1, "qt", lambda j: q_n[:, P * j:P * (j + 1)], q_tr)
                d_part(2, 3)
                heads(11, 12)
                d_part(3, 4)
                scores(3)
                heads(12, 13)
                ctx_part("k", wk_h, wk_l, 0, 2, k_mm)
                heads(13, 14)
                ctx_part("k", wk_h, wk_l, 2, 4, k_mm)
                heads(14, 15)
                y_part(0, 1)
                heads(15, 16)
                y_part(1, 2)
                scores(4)
                heads(16, 17)
                y_part(2, 3)
                heads(17, 18)
                y_part(3, 4)
                turn_maxima(1, 0, 1, "c0")
                heads(18, 19)
                values(0, 0)
                heads(19, 20)
                scores(5)
                heads(20, 21)
                ctx_part("v", wv_h, wv_l, 0, 1, v_mm)
                heads(21, 22)
                ctx_part("v", wv_h, wv_l, 1, 2, v_mm)
                heads(22, 24)
                scores(6)
                heads(24, 25)
                if has(-1):
                    pe.wait_ge(x1_ok, i)
                    turn4(0, "x1t", lambda j: x1[odd][:, P * j:P * (j + 1)], x1_tr)
                heads(25, 26)
                ctx_part("v", wv_h, wv_l, 2, 4, v_mm)
                heads(26, 27)
                xm_part(0, 2)
                heads(27, 28)
                xm_part(2, 3)
                scores(7)
                heads(28, 29)
                xm_part(3, 4)
                heads(29, 30)
                if has(-1):
                    pe.wait_ge(xm_ok, i)
                    turn4(0, "xmt", lambda j: xm_n[:, P * j:P * (j + 1)], xm_tr)
                heads(30, 32)
                s1_part(0, 2)
                s1_part(2, 4)

            run_steps(nc, pe, step, after)

        @block.vector
        def _(dve):
            st = pr[:, :, :, :].rearrange("p a b c -> p (a b c)")
            V = nc.vector
            dve.wait_ge(prep_act, 1)
            V.tensor_tensor(wq_l[:, :, :].rearrange("p a b -> p (a b)"), st[:, 0:2048],
                            wq_h[:, :, :].rearrange("p a b -> p (a b)").bitcast(F32), ALU.subtract).then_inc(prep_dve, 1)
            dve.wait_ge(prep_act, 2)
            V.tensor_tensor(wk_l[:, :, :].rearrange("p a b -> p (a b)"), st[:, 2048:2560],
                            wk_h[:, :, :].rearrange("p a b -> p (a b)").bitcast(F32), ALU.subtract).then_inc(prep_dve, 1)
            dve.wait_ge(prep_act, 3)
            V.tensor_tensor(wv_l[:, :, :].rearrange("p a b -> p (a b)"), st[:, 2560:3072],
                            wv_h[:, :, :].rearrange("p a b -> p (a b)").bitcast(F32), ALU.subtract).then_inc(prep_dve, 1)
            dve.wait_ge(w_in[1], 128)
            dve.wait_ge(prep_pool, 1)
            V.tensor_scalar(bv_b[:, :], ones[:, :], bv_c[:, 0:1], None, ALU.mult).then_inc(prep_dve, 1)
            V.memset(half_c[:, :], -0.5).then_inc(prep_dve, 1)
            dve.wait_ge(prep_pe, 1)
            V.tensor_copy(bo_b[:, :], o_ps[0:L, :]).then_inc(prep_dve, 1)

            def after(i):
                if i == STEPS[0]:
                    for t in range(KT):
                        dve.wait_ge(prep_act, 3 + t + 1)
                        src = sc_ps[:, t, :] if t < SC else o_ps[:, :]
                        V.scalar_tensor_tensor(m_l[:, t, :], src, float(H) ** -0.5, m_h[:, t, :].bitcast(F32),
                                               ALU.mult, ALU.subtract).then_inc(prep_dve, 1)

            def step(i, par, has):
                odd = 1 - par

                def add_mask(g):
                    if not has(0):
                        return
                    b = i
                    if g == 0:
                        dve.wait_ge(mt_in[par], ring(b, par))
                    if g == 0:
                        wait(dve, pv_mm, 2 * b)
                    if g == 4:
                        dve.wait_ge(pv_mm, 2 * b + 1)
                    for c in range(2):
                        dve.wait_ge(sc_mm, 24 * b + 3 * g + c + 1)
                        V.tensor_tensor(pr[:, g % 4, c, :].rearrange("p (j l) -> p j l", j=J),
                                        sc_ps[:, c, 0:JL].rearrange("p (j l) -> p j l", j=J),
                                        mask_t[par][:, c, :].unsqueeze(1).to_broadcast([P, J, L]),
                                        ALU.add).then_inc(sc_add, 1)

                def maxima(n0, n1):
                    if not has(1):
                        return
                    b = i + 1
                    if n0 == 0:
                        dve.wait_ge(mn_in[odd], ring(b, odd))
                        wait(dve, m_tr, 2 * (b - 1))
                    for n in range(n0, n1):
                        hold(dve, a_mm, NH * b + n + 1)
                        src = mx_ps[0:L, n % 2, 0:S]
                        V.tensor_tensor_reduce(out=src, in0=src, in1=mask_n[odd][:, :], scale=1.0, scalar=-3.0e38,
                                               op0=ALU.add, op1=ALU.max,
                                               accum_out=mx[odd][:, n:n + 1]).then_inc(a_mx, 1)

                def maxima_low(b, half, w):
                    dve.wait_ge(mh_ok, 2 * b + half + 1)
                    wait(dve, m_in[half], 32 * b)
                    V.scalar_tensor_tensor(mt_l[half][:, :], work[0:16, w, 0:L], -1.0, mt_h[half][:, :].bitcast(F32),
                                           ALU.mult, ALU.subtract).then_inc(ml_ok, 1)

                def normalise(j):
                    if not has(-1):
                        return
                    b, cols = i - 1, slice(L * j, L * (j + 1))
                    if j == 0:
                        dve.wait_ge(ot_in, 32 * (b + 1))
                    V.reciprocal(r_b[:, cols], r_b[:, cols]).then_inc(r_ok, 1)
                    dve.wait_ge(r_ok, J * b + j + 1)
                    V.tensor_tensor(o_n[:, cols], o_n[:, cols], r_b[:, cols], ALU.mult).then_inc(on_ok, 1)

                if has(-2):
                    b = i - 2
                    dve.wait_ge(s1_mm, b + 1)
                    wait(dve, p1_ok, b)
                    V.tensor_reduce(nm1[:, :], work[0:L, 0, 0:S], AX.X, ALU.max, negate=True).then_inc(nm_ok, 1)
                maxima(0, 2)
                if has(0):
                    maxima_low(i, 1, 1)
                if has(2):
                    b = i + 2
                    dve.wait_ge(xh_ok, b + 1)
                    wait(dve, q_mm, b)
                    wait(dve, xm_mm, i - 1)
                    V.tensor_tensor(x_l[:, :], xT[:, :], x_h[:, :].bitcast(F32), ALU.subtract).then_inc(xl_ok, 1)
                add_mask(0)
                maxima(2, 4)
                if has(-2):
                    b = i - 2
                    dve.wait_ge(p1_ok, b + 1)
                    wait(dve, ra_ok, b)
                    V.reciprocal(ra0[:, :], s1[:, :]).then_inc(ra0_ok, 1)
                    dve.wait_ge(ra0_ok, b + 1)
                    wait(dve, res_ok, b)
                    V.tensor_scalar(ra[:, :], ra0[:, :], alpha_c[:, 0:1], None, ALU.mult).then_inc(ra_ok, 1)
                add_mask(1)
                maxima(4, 8)
                if has(2):
                    b = i + 2
                    dve.wait_ge(q_mm, b + 1)
                    wait(dve, q_tr, b)
                    V.tensor_tensor(q_n[:, :], work[0:L, 1, :], bq_b[:, :], ALU.add).then_inc(q_nat, 1)
                add_mask(2)
                maxima(8, 9)
                normalise(0)
                maxima(9, 10)
                normalise(1)
                maxima(10, 11)
                if has(2):
                    b = i + 2
                    dve.wait_ge(qh_ok, b + 1)
                    wait(dve, q_out, 32 * b)
                    V.scalar_tensor_tensor(q_l[:, :], work[:, 1, 0:JL], 0.25, q_h[:, :].bitcast(F32),
                                           ALU.mult, ALU.subtract).then_inc(ql_ok, 1)
                normalise(2)
                maxima(11, 12)
                normalise(3)
                add_mask(3)
                if has(-2):
                    b = i - 2
                    dve.wait_ge(d_mm, b + 1)
                    dve.wait_ge(ra_ok, b + 1)
                    V.scalar_tensor_tensor(x1[par][:, :], work[0:L, 0, :], ra[:, 0:1], x1[par][:, :],
                                           ALU.mult, ALU.add).then_inc(res_ok, 1)
                maxima(12, 14)
                if has(2):
                    b = i + 2
                    dve.wait_ge(kh_ok, b + 1)
                    wait(dve, k_out, 32 * b)
                    V.scalar_tensor_tensor(k_l[:, :], work[:, 1, 0:SP2], bk_c[:, 0:1], k_h[:, :].bitcast(F32),
                                           ALU.add, ALU.subtract).then_inc(kl_ok, 1)
                maxima(14, 16)
                maxima(16, 18)
                if has(-1):
                    b = i - 1
                    dve.wait_ge(y_mm, b + 1)
                    dve.wait_ge(xb_ok, b + 1)
                    V.tensor_tensor(y[:, :], work[0:L, 0, :], y[:, :], ALU.add).then_inc(y_ok, 1)
                    dve.wait_ge(y_ok, b + 1)
                    V.bn_stats(stats[:, :], y[:, :]).then_inc(st_ok, 1)
                    dve.wait_ge(st_ok, b + 1)
                    hold(dve, ve_ok, b)
                    V.bn_aggr(mv[:, :], stats[:, :]).then_inc(mv_ok, 1)
                if has(1):
                    maxima_low(i + 1, 0, 1)
                maxima(18, 19)
                if has(-1):
                    b = i - 1
                    dve.wait_ge(rstd_ok, b + 1)
                    dve.wait_ge(mv_ok, b + 1)
                    V.tensor_scalar(y[:, :], y[:, :], mv[:, 0:1], rstd[:, 0:1], ALU.subtract, ALU.mult).then_inc(xc_ok, 1)
                add_mask(4)
                maxima(19, 20)
                add_mask(5)
                maxima(20, 24)
                add_mask(6)
                maxima(24, 25)
                if has(-1):
                    b = i - 1
                    dve.wait_ge(x1h_ok, b + 1)
                    wait(dve, xm_mm, b)
                    dve.wait_ge(q_mm, upto(i + 3))
                    V.tensor_tensor(x_l[:, :], work[:, 0, 0:JL], x_h[:, :].bitcast(F32), ALU.subtract).then_inc(x1l_ok, 1)
                maxima(25, 28)
                add_mask(7)
                maxima(28, 32)

            run_steps(nc, dve, step, after)

        @block.scalar
        def _(act):
            st = pr[:, :, :, :].rearrange("p a b c -> p (a b c)")
            A = nc.scalar
            act.wait_ge(w_in[0], 48)
            A.activation(wq_h[:, :, :].rearrange("p a b -> p (a b)"), st[:, 0:2048], ACT.Copy).then_inc(prep_act, 1)
            A.activation(wk_h[:, :, :].rearrange("p a b -> p (a b)"), st[:, 2048:2560], ACT.Copy).then_inc(prep_act, 1)
            A.activation(wv_h[:, :, :].rearrange("p a b -> p (a b)"), st[:, 2560:3072], ACT.Copy).then_inc(prep_act, 1)
            act.wait_ge(prep_act, 3)
            act.wait_ge(prep_dve, 3)
            act.dma_start(st[:, 0:2048], w1q_d).then_inc(w_in[2], 16)
            act.dma_start(st[:, 2048:4096], w1k_d).then_inc(w_in[2], 16)

            def after(i):
                n = i - STEPS[0]
                for t in range(KT):
                    act.wait_ge(prep_pe, 1 + KT * n + t + 1)
                    src = sc_ps[:, t, :] if t < SC else o_ps[:, :]
                    if n == 0:
                        A.activation(m_h[:, t, :], src, ACT.Copy, scale=float(H) ** -0.5).then_inc(prep_act, 1)
                    else:
                        A.activation(n_w[:, t, :], src, ACT.Copy).then_inc(prep_act, 1)

            def step(i, par, has):
                odd = 1 - par

                def copy_scores(g):
                    if not has(0):
                        return
                    b = i
                    act.wait_ge(sc_mm, 24 * b + 3 * g + 3)
                    if g == 0:
                        wait(act, pv_mm, 2 * b)
                    if g == 4:
                        act.wait_ge(pv_mm, 2 * b + 1)
                    A.activation(pr[:, g % 4, 2, :], sc_ps[:, 2, 0:JL], ACT.Copy).then_inc(sc_cp, 1)

                def probabilities(g):
                    if not has(0):
                        return
                    b = i
                    act.wait_ge(sc_add, 2 * (8 * b + g + 1))
                    act.wait_ge(sc_pool, 8 * b + g + 1)
                    t = pr[:, g % 4, :, :].rearrange("p c n -> p (c n)")
                    A.activation(t, t, ACT.Exp).then_inc(ex_ok, 1)

                def output(off, half):
                    if not has(off):
                        return
                    b = i + off
                    act.wait_ge(pv_mm, 2 * b + half + 1)
                    wait(act, os_out[half], 16 * b)
                    A.activation(o_s[half][:, :], o_ps[:, 0:JL], ACT.Copy).then_inc(os_ok, 1)

                def maxima_high(b, half, w):
                    act.wait_ge(m_tr, 2 * b + half + 1)
                    wait(act, m_in[half], 32 * b)
                    A.activation(mt_h[half][:, :], work[0:16, w, 0:L], ACT.Copy, scale=-1.0).then_inc(mh_ok, 1)

                if has(-2):
                    b = i - 2
                    act.wait_ge(nm_ok, b + 1)
                    wait(act, p1_tr, b)
                    wait(act, ra0_ok, b)
                    A.activation(p1[:, 0:S], work[0:L, 0, 0:S], ACT.Exp, bias=nm1[:, 0:1],
                                 accum_out=s1[:, :]).then_inc(p1_ok, 1)
                if has(0):
                    maxima_high(i, 1, 1)
                if has(2):
                    b = i + 2
                    act.wait_ge(x_in, 16 * (b + 1))
                    wait(act, q_mm, b)
                    wait(act, xl_ok, b)
                    wait(act, xm_mm, i - 1)
                    wait(act, x1l_ok, i - 1)
                    A.activation(x_h[:, :], xT[:, :], ACT.Copy).then_inc(xh_ok, 1)
                output(-1, 1)
                if has(1):
                    b = i + 1
                    act.wait_ge(v_tr, b + 1)
                    wait(act, pv_mm, 2 * (b - 1))
                    for c0, c1, k in ((0, 2, P), (2, 3, LAST)):
                        A.activation(va[odd][0:k, c0:c1, :, 0:HD].rearrange("p c g d -> p (c g) d"),
                                     work[0:k, 1, P * c0:P * c1].rearrange("p (n d) -> p n d", d=HD),
                                     ACT.Copy).then_inc(va_ok, 1)
                copy_scores(0)
                if has(-2):
                    b = i - 2
                    act.wait_ge(p1_tr, b + 1)
                    wait(act, cx_mm, b)
                    A.activation(p1_t[:, 0:2, :].rearrange("p c l -> p (c l)"), work[:, 0, 0:2 * L],
                                 ACT.Copy).then_inc(p1t_ok, 1)
                    A.activation(p1_t[0:LAST, 2, :], work[0:LAST, 0, 2 * L:3 * L], ACT.Copy).then_inc(p1t_ok, 1)
                if has(2):
                    b = i + 2
                    act.wait_ge(c_in, 16 * (b + 1))
                    wait(act, v_mm, b)
                    wait(act, cl_ok, b)
                    A.activation(c_h[:, :], cT[:, :], ACT.Copy).then_inc(ch_ok, 1)
                probabilities(0)
                copy_scores(1)
                probabilities(1)
                if has(-2):
                    b = i - 2
                    act.wait_ge(cx_mm, b + 1)
                    wait(act, d_mm, b)
                    act.wait_ge(s1_mm, b + 1)
                    A.activation(turned[:, :], work[:, 0, 0:JL], ACT.Copy).then_inc(cxt_ok, 1)
                copy_scores(2)
                if has(2):
                    b = i + 2
                    act.wait_ge(q_tr, b + 1)
                    wait(act, q_out, 32 * b)
                    wait(act, ql_ok, b)
                    A.activation(q_h[:, :], work[:, 1, 0:JL], ACT.Copy, scale=0.25).then_inc(qh_ok, 1)
                probabilities(2)
                copy_scores(3)
                if has(2):
                    b = i + 2
                    act.wait_ge(k_mm, b + 1)
                    wait(act, k_out, 32 * b)
                    wait(act, kl_ok, b)
                    A.activation(k_h[:, :], work[:, 1, 0:SP2], ACT.Identity, bias=bk_c[:, 0:1]).then_inc(kh_ok, 1)
                probabilities(3)
                if has(1):
                    maxima_high(i + 1, 0, 1)
                output(0, 0)
                copy_scores(4)
                probabilities(4)
                copy_scores(5)
                probabilities(5)
                if has(-1):
                    b = i - 1
                    act.wait_ge(x1_tr, b + 1)
                    act.wait_ge(q_mm, upto(i + 3))
                    act.wait_ge(xl_ok, upto(i + 3))
                    wait(act, xm_mm, b)
                    A.activation(x_h[:, :], work[:, 0, 0:JL], ACT.Copy).then_inc(x1h_ok, 1)
                copy_scores(6)
                if has(2):
                    b = i + 2
                    act.wait_ge(v_mm, b + 1)
                    wait(act, v_tr, b)
                    A.activation(vT[:, :], work[:, 1, 0:SP2], ACT.Copy).then_inc(vT_ok, 1)
                probabilities(6)
                if has(-1):
                    b = i - 1
                    act.wait_ge(xm_mm, b + 1)
                    wait(act, xm_tr, b)
                    A.activation(xm_n[:, :], work[0:L, 0, :], ACT.Copy).then_inc(xm_ok, 1)
                copy_scores(7)
                if has(-1):
                    b = i - 1
                    act.wait_ge(xm_tr, b + 1)
                    wait(act, s1_mm, b)
                    wait(act, d_mm, b)
                    A.activation(turned[:, :], work[:, 0, 0:JL], ACT.Copy).then_inc(xmt_ok, 1)
                probabilities(7)

            run_steps(nc, act, step, after)

        @block.gpsimd
        def _(pool):
            G = nc.gpsimd
            pool.memset(ones[:, :], 1.0).then_inc(prep_pool, 1)
            pool.memset(ident[:, :], 0.0).then_inc(prep_pool, 1)
            pool.wait_ge(prep_pool, 2)
            pool.affine_select(out=ident[:, :], in_=ident[:, :], compare_op=ALU.not_equal, fill=1.0, base=0,
                               pattern=[[-1, P]], channel_multiplier=1).then_inc(prep_pool, 1)
            for p in range(2):
                pool.wait_ge(prep_pool, 3 + 3 * p)
                pool.memset(ks[p][0:64, :, SP2:SC * P].bitcast(F32), 0.0).then_inc(prep_pool, 1)
                pool.wait_ge(prep_pool, 4 + 3 * p)
                pool.memset(va[p][:, :, :, HD:2 * HD], 1.0).then_inc(prep_pool, 1)
                pool.wait_ge(prep_pool, 5 + 3 * p)
                pool.memset(ks[p][64:66, :, 0:SC * P].bitcast(F32), 1.0).then_inc(prep_pool, 1)
            pool.wait_ge(prep_pool, 9)

            def step(i, par, has):
                odd = 1 - par

                def add_mask(g):
                    if not has(0):
                        return
                    b = i
                    if g == 0:
                        pool.wait_ge(mt_in[par], ring(b, par))
                    pool.wait_ge(sc_cp, 8 * b + g + 1)
                    t = pr[:, g % 4, 2, :].rearrange("p (j l) -> p j l", j=J)
                    G.tensor_tensor(t, t, mask_t[par][:, 2, :].unsqueeze(1).to_broadcast([P, J, L]),
                                    ALU.add).then_inc(sc_pool, 1)

                add_mask(0)
                if has(2):
                    b = i + 2
                    pool.wait_ge(ch_ok, b + 1)
                    wait(pool, v_mm, b)
                    G.tensor_tensor(c_l[:, :], cT[:, :], c_h[:, :].bitcast(F32), ALU.subtract).then_inc(cl_ok, 1)
                add_mask(1)
                if has(-1):
                    b = i - 1
                    pool.wait_ge(xn_in, 16 * (b + 1))
                    pool.wait_ge(prep_dve, 6)
                    G.tensor_tensor(y[:, :], y[:, :], bo_b[:, :], ALU.add).then_inc(xb_ok, 1)
                add_mask(2)
                add_mask(3)
                if has(-1):
                    b = i - 1
                    pool.wait_ge(mv_ok, b + 1)
                    hold(pool, rstd_ok, b)
                    G.tensor_scalar(ve[:, :], mv[:, 1:2], EPS, None, ALU.add).then_inc(ve_ok, 1)
                    pool.wait_ge(ve_ok, b + 1)
                    wait(pool, xc_ok, b)
                    G.tensor_tensor(rstd[:, :], ve[:, :], half_c[:, :], ALU.pow).then_inc(rstd_ok, 1)
                add_mask(4)
                if has(-1):
                    b = i - 1
                    pool.wait_ge(xc_ok, b + 1)
                    if not isinstance(b, int) or b >= 2:
                        pool.wait_ge(out_ok[odd], ring(b - 2, odd))
                    G.tensor_tensor(x1[odd][:, :], y[:, :], gamma_b[:, :], ALU.mult).then_inc(xg_ok, 1)
                    pool.wait_ge(xg_ok, b + 1)
                    G.tensor_tensor(x1[odd][:, :], x1[odd][:, :], beta_b[:, :], ALU.add).then_inc(x1_ok, 1)
                add_mask(5)
                add_mask(6)
                add_mask(7)

            run_steps(nc, pool, step)


_INS = ("xT", "x", "ctxT", "ctx", "mask", "maskT", "wq", "wk", "wv", "wo", "bq", "bk", "bv", "bo",
        "gamma", "beta", "w1q", "w1k", "w1v", "w1o", "alpha")


def kernel(**inputs):
    import numpy as np
    import concourse.bacc as bacc
    from concourse.bass_utils import run_bass_kernel_spmd as run

    a = {k: np.asarray(v) for k, v in inputs.items()}

    def rows(w):
        return w.reshape(KT, P, -1).transpose(1, 0, 2).reshape(P, -1)

    def by_head(w):
        return w.reshape(-1, KVH, J, HD).transpose(0, 2, 1, 3).reshape(-1, H)

    def chunks(t, size, pieces):
        t = np.pad(t, ((0, 0), (0, size * pieces - t.shape[1]), (0, 0)))
        return t.reshape(B, pieces, size, -1).transpose(0, 2, 1, 3)

    x, c, mask = a["x"], a["ctx_2048"], a["mask_Bx1xSxS2_ff0"][:, 0]
    cT = np.pad(c.transpose(0, 2, 1), ((0, 0), (0, 0), (0, SP2 - S)))
    arrays = {
        "xT": chunks(x.transpose(0, 2, 1), P, KT).reshape(B, P, -1),
        "x": x,
        "ctxT": chunks(cT, P, KT).reshape(B, P, -1),
        "ctx": chunks(c, P, SC),
        "mask": mask,
        "maskT": chunks(mask.transpose(0, 2, 1), P, SC),
        "wq": rows(by_head(a["L0_xattn_Wq"])),
        "wk": rows(a["L0_xattn_Wk"]),
        "wv": rows(a["L0_xattn_Wv"]),
        "wo": rows(a["L0_xattn_Wo"].reshape(KVH, J, HD, H).transpose(1, 0, 2, 3).reshape(H, H)),
        "bq": np.broadcast_to(by_head(a["L0_xattn_bq"].reshape(1, H)), (L, H)),
        "bk": a["L0_xattn_bk"].reshape(P, 1),
        "bv": a["L0_xattn_bv"].reshape(P, 1),
        "bo": a["L0_xattn_bo"].reshape(1, H),
        "gamma": np.broadcast_to(a["L0_xattn_gamma"], (L, H)),
        "beta": np.broadcast_to(a["L0_xattn_beta"], (L, H)),
        "w1q": rows(a["L1_xattn_w_q"]),
        "w1k": rows(a["L1_xattn_w_k"]),
        "w1v": rows(a["L1_xattn_w_v"]),
        "w1o": rows(a["L1_xattn_w_o"].T),
        "alpha": np.broadcast_to(a["L1_xattn_alpha"].reshape(1, 1), (L, 1)),
    }
    nc = bacc.Bacc("TRN2", target_bir_lowering=False, num_devices=1)
    feeds, args = {}, []
    for name in _INS:
        t = np.ascontiguousarray(arrays[name])
        feeds[f"in_{name}"] = t
        args.append(nc.dram_tensor(f"in_{name}", t.shape, mybir.dt.from_np(t.dtype), kind="ExternalInput").ap())
    args.append(nc.dram_tensor("out", (B, L, H), F32, kind="ExternalOutput").ap())
    build(nc, *args)
    return run(nc, [feeds], core_ids=[0]).results[0]["out"]
```

```python
from contextlib import ExitStack

import concourse.bass as bass
from concourse import mybir

F32 = mybir.dt.float32
F32R = mybir.dt.float32r
ACT = mybir.ActivationFunctionType
ALU = mybir.AluOpType
AX = mybir.AxisListType

B, L, S, H = 16, 100, 361, 512
NH, KVH, HD = 32, 8, 16
J = NH // KVH
P = 128
KT = H // P
SP2 = S + 1
SC = 3
LAST = S - 2 * P
JL = J * L
EPS = 1e-6

LOOP = (2, 14)
STEPS = (-2, B + 2)

BANK_USERS = (
    (("p1t", -2, "p1t_ok", 2, 2), ("cx", -2, "cxt_ok", 1, 1), ("d", -2, "res_ok", 1, 1),
     ("y", -1, "y_ok", 1, 1), ("c0", 1, "ml_ok", 2, 1), ("x1t", -1, "x1l_ok", 1, 1),
     ("xm", -1, "xm_ok", 1, 1), ("xmt", -1, "xmt_ok", 1, 1), ("s1", -1, "p1_ok", 1, 1)),
    (("c1", 0, "ml_ok", 2, 2), ("vt", 1, "va_ok", 2, 2), ("q", 2, "q_nat", 1, 1),
     ("qt", 2, "ql_ok", 1, 1), ("k", 2, "kl_ok", 1, 1), ("v", 2, "vT_ok", 1, 1)),
)


def in_range(batch):
    return 0 <= batch < B


def upto(count):
    return min(count, B) if isinstance(count, int) else count


def emptied(bank, piece, i):
    users = BANK_USERS[bank]
    at = [user[0] for user in users].index(piece)
    for back in range(1, 3 * len(users)):
        behind, before = divmod(at - back, len(users))
        _, off, name, each, done = users[before]
        batch = i + behind + off
        if not isinstance(i, int) or in_range(batch):
            return name, each * batch + done
    return None, 0


def wait(eng, sem, value):
    if not (isinstance(value, int) and value <= 0):
        eng.wait_ge(sem, value)


def hold(eng, sem, value):
    wait(eng, sem, value)
    if not isinstance(value, int):
        eng.nop(nofuse=True)


def ring(b, par, dmas=1):
    return (8 * b - 8 * par + 16) * dmas


def run_steps(nc, eng, body, after=None):
    for i in range(STEPS[0], LOOP[0]):
        body(i, i % 2, lambda off, i=i: in_range(i + off))
        if after and i < 0:
            after(i)
    with eng.Fori(LOOP[0], LOOP[1], 2) as i:
        i = nc.s_assert_within(i, LOOP[0], LOOP[1] - 2,
                               skip_runtime_bounds_check_because="the loop goes by two and its range is even")
        body(i, 0, lambda off: True)
        body(i + 1, 1, lambda off: True)
    for i in range(LOOP[1], STEPS[1]):
        body(i, i % 2, lambda off, i=i: in_range(i + off))


def build(nc, xT_d, x_d, ctxT_d, ctx_d, mask_d, maskT_d, wq_d, wk_d, wv_d, wo_d, bq_d, bk_d, bv_d,
          bo_d, gamma_d, beta_d, w1q_d, w1k_d, w1v_d, w1o_d, alpha_d, out_d):
    with ExitStack() as ctx:
        def sb(name, shape, dt=F32):
            return ctx.enter_context(nc.sbuf_tensor(name, shape, dt))

        def sem(name):
            return ctx.enter_context(nc.semaphore(name))

        sc_ps = ctx.enter_context(nc.psum_tensor("sc_ps", [P, SC, 512], F32))
        mx_ps = ctx.enter_context(nc.psum_tensor("mx_ps", [P, 2, 512], F32))
        o_ps = ctx.enter_context(nc.psum_tensor("o_ps", [P, 512], F32))
        work = ctx.enter_context(nc.psum_tensor("work", [P, 2, 512], F32))

        wq_h, wq_l = sb("wq_h", [P, KT, H], F32R), sb("wq_l", [P, KT, H], F32R)
        wk_h, wk_l = sb("wk_h", [P, KT, P], F32R), sb("wk_l", [P, KT, P], F32R)
        wv_h, wv_l = sb("wv_h", [P, KT, P], F32R), sb("wv_l", [P, KT, P], F32R)
        m_h, m_l = sb("m_h", [P, KT, H], F32R), sb("m_l", [P, KT, H], F32R)
        n_w = sb("n_w", [P, KT, H])
        wo_h, wo_l = sb("wo_h", [P, J, H], F32R), sb("wo_l", [P, J, H], F32R)
        bq_b, gamma_b, beta_b, bo_b = (sb(n, [L, H]) for n in ("bq_b", "gamma_b", "beta_b", "bo_b"))
        bk_c, bv_c = sb("bk_c", [P, 1]), sb("bv_c", [P, 1])
        bo_r = sb("bo_r", [1, H])
        alpha_c = sb("alpha_c", [L, 1])
        half_c = sb("half_c", [L, 1])
        ident = sb("ident", [P, P])
        ones = sb("ones", [P, L])
        bv_b = sb("bv_b", [P, L])

        xT = sb("xT", [P, KT * L])
        cT = sb("cT", [P, KT * SP2])
        x_h, x_l = sb("x_h", [P, JL], F32R), sb("x_l", [P, JL], F32R)
        c_h, c_l = sb("c_h", [P, KT * SP2], F32R), sb("c_l", [P, KT * SP2], F32R)
        row_n = sb("row_n", [L, H])
        k_h, k_l = sb("k_h", [P, SP2], F32R), sb("k_l", [P, SP2], F32R)
        vT = sb("vT", [P, SP2])
        va = [sb(f"va{p}", [P, SC, KVH, 2 * HD]) for p in range(2)]
        qs = [sb(f"qs{p}", [66, KVH, JL], F32R) for p in range(2)]
        ks = [sb(f"ks{p}", [66, KVH, SC * P], F32R) for p in range(2)]
        mask_n = [sb(f"mask_n{p}", [L, S]) for p in range(2)]
        mx = [sb(f"mx{p}", [L, NH]) for p in range(2)]
        mt_h = [sb(f"mt_h{h}", [NH // 2, L], F32R) for h in range(2)]
        mt_l = [sb(f"mt_l{h}", [NH // 2, L], F32R) for h in range(2)]

        mask_t = [sb(f"mask_t{p}", [P, SC, L]) for p in range(2)]
        pr = sb("pr", [P, 4, SC, JL])
        o_s = sb("o_s", [P, JL])

        r_b = sb("r_b", [P, JL])
        o_h = sb("o_h", [P, JL], F32R)
        o_l = sb("o_l", [P, JL], F32R)
        den, rden = sb("den", [NH, L]), sb("rden", [NH, L])
        y = sb("y", [L, H])
        stats, mv, ve, rstd = sb("stats", [L, 6]), sb("mv", [L, 2]), sb("ve", [L, 1]), sb("rstd", [L, 1])
        x1 = [sb(f"x1_{p}", [L, H]) for p in range(2)]
        nm1, s1, ra0, ra = sb("nm1", [L, 1]), sb("s1", [L, 1]), sb("ra0", [L, 1]), sb("ra", [L, 1])
        p1, p1_t = sb("p1", [L, SP2]), sb("p1_t", [P, SC, L])
        ctx_n = sb("ctx_n", [P, SC, H])
        turned = sb("turned", [P, JL])

        k_dr = nc.dram_tensor("k_dr", (2, 2, P, SP2), F32, kind="Internal").ap()
        q_dr = nc.dram_tensor("q_dr", (2, 2, P, JL), F32, kind="Internal").ap()
        r_dr = nc.dram_tensor("r_dr", (NH, L), F32, kind="Internal").ap()
        o_dr = nc.dram_tensor("o_dr", (2, KVH * 32, JL), F32, kind="Internal").ap()

        w_in = [sem(f"w_in{n}") for n in range(5)]
        prep_act, prep_dve, prep_pool, prep_pe = sem("prep_act"), sem("prep_dve"), sem("prep_pool"), sem("prep_pe")
        x_in = sem("x_in")
        c_in = sem("c_in")
        c4_in = sem("c4_in")
        xh_ok, xl_ok, ch_ok, cl_ok = (sem(n) for n in ("xh_ok", "xl_ok", "ch_ok", "cl_ok"))
        q_mm, q_nat, q_tr, qh_ok, ql_ok = (sem(n) for n in ("q_mm", "q_nat", "q_tr", "qh_ok", "ql_ok"))
        k_mm, kh_ok, kl_ok = sem("k_mm"), sem("kh_ok"), sem("kl_ok")
        v_mm, vT_ok, v_tr, va_ok = sem("v_mm"), sem("vT_ok"), sem("v_tr"), sem("va_ok")
        k_out, q_out = sem("k_out"), sem("q_out")
        st_in = [sem(f"st_in{h}") for h in range(2)]
        mn_in = [sem(f"mn_in{p}") for p in range(2)]
        mt_in = [sem(f"mt_in{p}") for p in range(2)]
        a_mm, a_mx = sem("a_mm"), sem("a_mx")
        m_tr, mh_ok, ml_ok = sem("m_tr"), sem("mh_ok"), sem("ml_ok")
        m_in = [sem(f"m_in{h}") for h in range(2)]
        sc_mm = sem("sc_mm")
        sc_add, sc_cp, sc_pool = sem("sc_add"), sem("sc_cp"), sem("sc_pool")
        ex_ok = sem("ex_ok")
        pv_mm, os_ok = sem("pv_mm"), sem("os_ok")
        os_out = [sem(f"os_out{h}") for h in range(2)]
        dn_in, ot_in, rd_out, rb_in = sem("dn_in"), sem("ot_in"), sem("rd_out"), sem("rb_in")
        rd_ok, on_ok, oh_ok, ol_ok = sem("rd_ok"), sem("on_ok"), sem("oh_ok"), sem("ol_ok")
        xn_in, xb_ok = sem("xn_in"), sem("xb_ok")
        y_mm, y_ok, st_ok, mv_ok, ve_ok, rstd_ok, xc_ok, xg_ok, x1_ok = (
            sem(n) for n in ("y_mm", "y_ok", "st_ok", "mv_ok", "ve_ok", "rstd_ok", "xc_ok", "xg_ok", "x1_ok"))
        x1_tr, x1h_ok, x1l_ok = sem("x1_tr"), sem("x1h_ok"), sem("x1l_ok")
        xm_mm, xm_ok, xm_tr, xmt_ok = sem("xm_mm"), sem("xm_ok"), sem("xm_tr"), sem("xmt_ok")
        s1_mm, nm_ok, p1_ok, ra0_ok, ra_ok = (sem(n) for n in ("s1_mm", "nm_ok", "p1_ok", "ra0_ok", "ra_ok"))
        p1_tr, p1t_ok, cn_in, cx_mm, cxt_ok = (sem(n) for n in ("p1_tr", "p1t_ok", "cn_in", "cx_mm", "cxt_ok"))
        d_mm, res_ok = sem("d_mm"), sem("res_ok")
        out_ok = [sem(f"out_ok{p}") for p in range(2)]

        block = ctx.enter_context(nc.Block())

        @block.sync
        def _(sp):
            st = pr[:, :, :, :].rearrange("p a b c -> p (a b c)")
            sp.dma_start(n_w[:, :, :].rearrange("p a b -> p (a b)"), wq_d).then_inc(w_in[0], 16)
            sp.dma_start(ctx_n[:, 0, :], wk_d).then_inc(w_in[0], 16)
            sp.dma_start(ctx_n[:, 1, :], wv_d).then_inc(w_in[0], 16)
            sp.dma_start(bk_c[:, :], bk_d).then_inc(w_in[1], 16)
            sp.dma_start(bv_c[:, :], bv_d).then_inc(w_in[1], 16)
            sp.dma_start(bq_b[:, :], bq_d).then_inc(w_in[1], 16)

            def after(i):
                if i == STEPS[0]:
                    sp.wait_ge(prep_pe, 4)
                    sp.dma_start(st[:, 0:2048], w1v_d).then_inc(w_in[3], 16)
                    sp.dma_start(st[:, 2048:4096], w1o_d).then_inc(w_in[3], 16)

            def step(i, par, has):
                odd = 1 - par

                def stack_in(b, p, half, parts=range(4)):
                    gs = slice(4 * half, 4 * half + 4)
                    for r in parts:
                        sp.dma_start(ks[p][HD * r:HD * (r + 1), gs, 0:SP2].bitcast(F32),
                                     k_dr[p, r // 2, :, :].rearrange("(g d) s -> d g s", d=HD)[:, gs, :]
                                     ).then_inc(st_in[half], 16)
                        sp.dma_start(qs[p][HD * r:HD * (r + 1), gs, :].bitcast(F32),
                                     q_dr[p, r % 2, :, :].rearrange("(g d) c -> d g c", d=HD)[:, gs, :]
                                     ).then_inc(st_in[half], 16)

                def maxima_in(b, half, stack):
                    hold(sp, mh_ok, 2 * b + half + 1)
                    hold(sp, ml_ok, 2 * b + half + 1)
                    for row, t in ((64, mt_h[half]), (65, mt_l[half])):
                        dst = stack[row:row + 1, 4 * half:4 * half + 4, :].bitcast(F32).rearrange(
                            "p g (j l) -> p (g j) l", j=J)
                        sp.dma_start(dst, t[:, :].bitcast(F32)).then_inc(m_in[half], 16)

                if has(2):
                    b = i + 2
                    hold(sp, xh_ok, b)
                    hold(sp, xl_ok, b)
                    sp.dma_start(xT[:, :], xT_d[b, :, :]).then_inc(x_in, 16)
                    hold(sp, ch_ok, b)
                    hold(sp, cl_ok, b)
                    hold(sp, s1_mm, i - 1)
                    sp.dma_start(cT[:, :], ctxT_d[b, :, :]).then_inc(c_in, 16)
                if has(0):
                    maxima_in(i, 1, qs[par])
                if has(-1):
                    b = i - 1
                    hold(sp, os_ok, 2 * b + 2)
                    sp.dma_start(o_dr[odd, P:2 * P, :], o_s[:, :]).then_inc(os_out[1], 16)
                    hold(sp, xg_ok, b)
                    sp.dma_start(y[:, :], x_d[b, :, :]).then_inc(xn_in, 16)
                if has(2):
                    b = i + 2
                    hold(sp, a_mx, NH * (i + 1))
                    sp.dma_start(mask_n[par][:, :], mask_d[b, :, :]).then_inc(mn_in[par], 16)
                if has(-1):
                    b = i - 1
                    hold(sp, os_out[0], 16 * (b + 1))
                    hold(sp, os_out[1], 16 * (b + 1))
                    hold(sp, rd_ok, b)
                    rows = o_dr[odd, :, :].rearrange("(g r) c -> g r c", r=2 * HD)
                    sp.dma_start(den[:, :], rows[:, HD, :].rearrange("g (j l) -> g j l", j=J)).then_inc(dn_in, 16)
                    hold(sp, y_mm, b)
                    sp.dma_start(o_l[:, :].bitcast(F32), rows[:, 0:HD, :]).then_inc(ot_in, 16)
                if has(1):
                    hold(sp, sc_mm, 24 * i)
                    stack_in(i + 1, odd, 1, (0, 1))
                if has(-1):
                    b = i - 1
                    hold(sp, rd_ok, b + 1)
                    sp.dma_start(r_dr[:, :], rden[:, :]).then_inc(rd_out, 16)
                if has(1):
                    stack_in(i + 1, odd, 1, (2, 3))
                if has(-1):
                    b = i - 1
                    hold(sp, oh_ok, b)
                    hold(sp, ol_ok, b)
                    hold(sp, rd_out, 16 * (b + 1))
                    src = r_dr[:, :].rearrange("(g j) l -> g (j l)", j=J).unsqueeze(1).to_broadcast([KVH, HD, JL])
                    sp.dma_start(r_b[:, :], src).then_inc(rb_in, 16)
                if has(1):
                    hold(sp, sc_add, 8 * i)
                    hold(sp, sc_pool, 8 * i)
                    sp.dma_start(mask_t[odd][:, :, :], maskT_d[i + 1, :, :, :]).then_inc(mt_in[odd], 16)
                if has(-1):
                    b = i - 1
                    hold(sp, ch_ok, upto(i + 3))
                    hold(sp, cl_ok, upto(i + 3))
                    hold(sp, s1_mm, b)
                    sp.dma_start(cT[:, :], ctxT_d[b, :, :]).then_inc(c4_in, 16)
                    hold(sp, cx_mm, b)
                    sp.dma_start(ctx_n[:, :, :], ctx_d[b, :, :, :]).then_inc(cn_in, 16)
                if has(-2):
                    b = i - 2
                    hold(sp, res_ok, b + 1)
                    sp.dma_start(out_d[b, :, :], x1[par][:, :]).then_inc(out_ok[par], 16)
                if has(2):
                    b = i + 2
                    hold(sp, qh_ok, b + 1)
                    hold(sp, ql_ok, b + 1)
                    hold(sp, st_in[1], 128 * (b - 1))
                    sp.dma_start(q_dr[par, 0, :, :], x_h[:, :].bitcast(F32)).then_inc(q_out, 16)
                    sp.dma_start(q_dr[par, 1, :, :], x_l[:, :].bitcast(F32)).then_inc(q_out, 16)
                    hold(sp, kh_ok, b + 1)
                    hold(sp, kl_ok, b + 1)
                    sp.dma_start(k_dr[par, 0, :, :], k_h[:, :].bitcast(F32)).then_inc(k_out, 16)
                    sp.dma_start(k_dr[par, 1, :, :], k_l[:, :].bitcast(F32)).then_inc(k_out, 16)
                if has(1):
                    maxima_in(i + 1, 0, qs[odd])
                if has(0):
                    hold(sp, os_ok, 2 * i + 1)
                    hold(sp, ot_in, 16 * (i - 1))
                    sp.dma_start(o_dr[par, 0:P, :], o_s[:, :]).then_inc(os_out[0], 16)
                if has(2):
                    b = i + 2
                    hold(sp, q_out, 32 * (b + 1))
                    hold(sp, k_out, 32 * (b + 1))
                    hold(sp, sc_mm, 24 * i + 12)
                    stack_in(b, par, 0)

            run_steps(nc, sp, step, after)
            for p in range(2):
                sp.wait_ge(out_ok[p], 16 * (B // 2))

        @block.tensor
        def _(pe):
            bank_read = dict(p1t_ok=p1t_ok, cxt_ok=cxt_ok, res_ok=res_ok, ml_ok=ml_ok, va_ok=va_ok, x1l_ok=x1l_ok,
                             xmt_ok=xmt_ok, p1_ok=p1_ok, q_nat=q_nat, kl_ok=kl_ok, ql_ok=ql_ok, vT_ok=vT_ok,
                             y_ok=y_ok, xm_ok=xm_ok)
            st = pr[:, :, :, :].rearrange("p a b c -> p (a b c)")
            pe.wait_ge(prep_pool, 9)
            pe.wait_ge(prep_dve, 3)

            def after(i):
                if i == STEPS[0]:
                    pe.wait_ge(w_in[4], 80)
                    pe.wait_ge(prep_dve, 4)
                    for j in range(J):
                        nc.tensor.matmul(mx_ps[0:L, 0, :], bv_b[:, :], n_w[:, j, :], start=(j == 0), stop=False)
                    nc.tensor.matmul(mx_ps[0:L, 0, :], ones[0:1, :], bo_r[:, :], start=False,
                                     stop=True).then_inc(prep_pe, 1)
                    pe.wait_ge(prep_dve, 10)
                else:
                    pe.wait_ge(prep_dve, 11)
                    pe.wait_ge(prep_act, 12)

            def product(dst, lh, ll, rh, rl, k, last):
                nc.tensor.matmul(dst, lh, rh, start=(k == 0), stop=False)
                nc.tensor.matmul(dst, lh, rl, start=False, stop=False)
                return nc.tensor.matmul(dst, ll, rh, start=False, stop=(k == last))

            def step(i, par, has):
                odd = 1 - par

                def bank(w, piece):
                    name, count = emptied(w, piece, i)
                    wait(pe, bank_read.get(name), count)
                    return work[:, w, :]

                def scores(g):
                    if not has(0):
                        return
                    b = i
                    if g == 0:
                        pe.wait_ge(m_in[0], 32 * (b + 1))
                    if g == KVH // 2:
                        pe.wait_ge(m_in[1], 32 * (b + 1))
                    for c in range(SC):
                        if c == 0:
                            wait(pe, sc_add, 8 * b + g)
                        else:
                            wait(pe, sc_cp, 8 * b + g)
                        nc.tensor.matmul(sc_ps[:, c, 0:JL], ks[par][:, g, P * c:P * (c + 1)], qs[par][:, g, :],
                                         start=True, stop=True).then_inc(sc_mm, 1)

                def heads(n0, n1):
                    if not has(1):
                        return
                    b = i + 1
                    for n in range(n0, n1):
                        g, j = n // J, n % J
                        if n % (NH // 2) == 0:
                            pe.wait_ge(st_in[n // (NH // 2)], 128 * (b + 1))
                        wait(pe, a_mx, NH * b + n - 1)
                        nc.tensor.matmul(mx_ps[0:L, n % 2, 0:SP2], qs[odd][0:64, g, L * j:L * (j + 1)],
                                         ks[odd][0:64, g, 0:SP2], start=True, stop=True).then_inc(a_mm, 1)

                def values(off, half):
                    if not has(off):
                        return
                    b, p = i + off, (par + off) % 2
                    pe.wait_ge(ex_ok, 8 * b + 4 * half + 4)
                    if half == 0:
                        pe.wait_ge(va_ok, 2 * (b + 1))
                    wait(pe, os_ok, 2 * b + half)
                    for c in range(SC):
                        k = P if c < 2 else LAST
                        for q in range(4):
                            mm = nc.tensor.matmul(o_ps[32 * q:32 * (q + 1), 0:JL], va[p][0:k, c, 4 * half + q, :],
                                                  pr[0:k, q, c, :], start=(c == 0), stop=(c == SC - 1))
                    mm.then_inc(pv_mm, 1)

                def turn_maxima(off, half, w, piece):
                    if not has(off):
                        return
                    b, p = i + off, (par + off) % 2
                    pe.wait_ge(a_mx, NH * b + 16 * (half + 1))
                    dst = bank(w, piece)
                    nc.tensor.matmul(dst[0:16, 0:L], mx[p][:, 16 * half:16 * half + 16], ident[0:L, 0:L],
                                     is_transpose=True, start=True, stop=True).then_inc(m_tr, 1)

                def turn4(w, piece, src, done):
                    dst = bank(w, piece)
                    for j in range(KT):
                        mm = nc.tensor.matmul(dst[:, L * j:L * (j + 1)], src(j), ident[0:L, 0:L],
                                              is_transpose=True, start=True, stop=True)
                    mm.then_inc(done, 1)

                def q_part(k0, k1):
                    if not has(2):
                        return
                    if k0 == 0:
                        pe.wait_ge(xh_ok, i + 3)
                        pe.wait_ge(xl_ok, i + 3)
                        bank(1, "q")
                    for k in range(k0, k1):
                        xs = slice(L * k, L * (k + 1))
                        mm = product(work[0:L, 1, :], x_h[:, xs], x_l[:, xs], wq_h[:, k, :], wq_l[:, k, :], k, KT - 1)
                    if k1 == KT:
                        mm.then_inc(q_mm, 1)

                def ctx_part(piece, w_h, w_l, k0, k1, done):
                    if not has(2):
                        return
                    if k0 == 0:
                        pe.wait_ge(ch_ok, i + 3)
                        pe.wait_ge(cl_ok, i + 3)
                        bank(1, piece)
                    for k in range(k0, k1):
                        cs = slice(SP2 * k, SP2 * (k + 1))
                        mm = product(work[:, 1, 0:SP2], w_h[:, k, :], w_l[:, k, :], c_h[:, cs], c_l[:, cs], k, KT - 1)
                    if k1 == KT:
                        mm.then_inc(done, 1)

                def cx_part(t0, t1):
                    if not has(-2):
                        return
                    if t0 == 0:
                        pe.wait_ge(p1t_ok, 2 * (i - 1))
                        pe.wait_ge(cn_in, 16 * (i - 1))
                        bank(0, "cx")
                    for t in range(t0, t1):
                        for c in range(SC):
                            k = P if c < 2 else LAST
                            mm = nc.tensor.matmul(work[:, 0, L * t:L * (t + 1)], ctx_n[0:k, c, P * t:P * (t + 1)],
                                                  p1_t[0:k, c, :], start=(c == 0), stop=(c == SC - 1))
                    if t1 == KT:
                        mm.then_inc(cx_mm, 1)

                def d_part(k0, k1):
                    if not has(-2):
                        return
                    if k0 == 0:
                        pe.wait_ge(cxt_ok, i - 1)
                        bank(0, "d")
                    for k in range(k0, k1):
                        mm = nc.tensor.matmul(work[0:L, 0, :], turned[:, L * k:L * (k + 1)], n_w[:, k, :],
                                              start=(k == 0), stop=(k == KT - 1))
                    if k1 == KT:
                        mm.then_inc(d_mm, 1)

                def y_part(j0, j1):
                    if not has(-1):
                        return
                    if j0 == 0:
                        pe.wait_ge(oh_ok, i)
                        pe.wait_ge(ol_ok, i)
                        bank(0, "y")
                    for j in range(j0, j1):
                        xs = slice(L * j, L * (j + 1))
                        mm = product(work[0:L, 0, :], o_h[:, xs], o_l[:, xs], wo_h[:, j, :], wo_l[:, j, :], j, J - 1)
                    if j1 == J:
                        mm.then_inc(y_mm, 1)

                def xm_part(k0, k1):
                    if not has(-1):
                        return
                    if k0 == 0:
                        pe.wait_ge(x1h_ok, i)
                        pe.wait_ge(x1l_ok, i)
                        bank(0, "xm")
                    for k in range(k0, k1):
                        xs = slice(L * k, L * (k + 1))
                        mm = product(work[0:L, 0, :], x_h[:, xs], x_l[:, xs], m_h[:, k, :], m_l[:, k, :], k, KT - 1)
                    if k1 == KT:
                        mm.then_inc(xm_mm, 1)

                def s1_part(k0, k1):
                    if not has(-1):
                        return
                    if k0 == 0:
                        pe.wait_ge(xmt_ok, i)
                        pe.wait_ge(c4_in, 16 * i)
                        bank(0, "s1")
                    for k in range(k0, k1):
                        mm = nc.tensor.matmul(work[0:L, 0, 0:SP2], turned[:, L * k:L * (k + 1)],
                                              cT[:, SP2 * k:SP2 * (k + 1)], start=(k == 0), stop=(k == KT - 1))
                    if k1 == KT:
                        mm.then_inc(s1_mm, 1)

                def fold_row(t):
                    if not isinstance(i, int) or i >= 0:
                        return
                    n = i - STEPS[0]
                    dst = sc_ps[:, t, :] if t < SC else o_ps[:, :]
                    pe.wait_ge(w_in[2 + n], 32)
                    if n == 1:
                        pe.wait_ge(prep_act, 3 + t + 1)
                        pe.wait_ge(prep_dve, 5 + t + 1)
                    for o in range(KT):
                        mm = nc.tensor.matmul(dst, st[:, 512 * o + P * t:512 * o + P * (t + 1)],
                                              st[:, 2048 + 512 * o:2048 + 512 * (o + 1)],
                                              start=(o == 0), stop=(o == KT - 1))
                    mm.then_inc(prep_pe, 1)

                def turn_p1():
                    if not has(-2):
                        return
                    pe.wait_ge(p1_ok, i - 1)
                    bank(0, "p1t")
                    for c in range(SC):
                        k = P if c < 2 else LAST
                        mm = nc.tensor.matmul(work[0:k, 0, L * c:L * (c + 1)], p1[:, P * c:P * c + k], ident[0:L, 0:L],
                                              is_transpose=True, start=True, stop=True)
                    mm.then_inc(p1_tr, 1)

                def turn_v():
                    if not has(1):
                        return
                    pe.wait_ge(vT_ok, i + 2)
                    bank(1, "vt")
                    for c in range(SC):
                        k = P if c < 2 else LAST
                        mm = nc.tensor.matmul(work[0:k, 1, P * c:P * (c + 1)], vT[:, P * c:P * c + k], ident[:, :],
                                              is_transpose=True, start=True, stop=True)
                    mm.then_inc(v_tr, 1)

                scores(0)
                heads(0, 2)
                turn_maxima(0, 1, 1, "c1")
                values(-1, 1)
                turn_v()
                heads(2, 4)
                turn_p1()
                q_part(0, 1)
                heads(4, 5)
                q_part(1, 2)
                heads(5, 6)
                q_part(2, 3)
                heads(6, 7)
                q_part(3, 4)
                heads(7, 8)
                scores(1)
                cx_part(0, 2)
                fold_row(0)
                heads(8, 9)
                cx_part(2, 4)
                heads(9, 10)
                scores(2)
                if has(2):
                    pe.wait_ge(q_nat, i + 3)
                    turn4(1, "qt", lambda j: row_n[:, P * j:P * (j + 1)], q_tr)
                fold_row(1)
                heads(10, 11)
                d_part(0, 2)
                heads(11, 12)
                d_part(2, 3)
                heads(12, 13)
                d_part(3, 4)
                scores(3)
                heads(13, 14)
                ctx_part("k", wk_h, wk_l, 0, 2, k_mm)
                heads(14, 15)
                y_part(0, 1)
                heads(15, 16)
                y_part(1, 2)
                heads(16, 17)
                y_part(2, 3)
                heads(17, 18)
                y_part(3, 4)
                heads(18, 19)
                scores(4)
                ctx_part("k", wk_h, wk_l, 2, 4, k_mm)
                fold_row(2)
                heads(19, 20)
                values(0, 0)
                turn_maxima(1, 0, 0, "c0")
                heads(20, 21)
                ctx_part("v", wv_h, wv_l, 0, 2, v_mm)
                heads(21, 22)
                fold_row(3)
                ctx_part("v", wv_h, wv_l, 2, 3, v_mm)
                if has(-1):
                    pe.wait_ge(x1_ok, i)
                    turn4(0, "x1t", lambda j: x1[odd][:, P * j:P * (j + 1)], x1_tr)
                scores(5)
                heads(22, 23)
                ctx_part("v", wv_h, wv_l, 3, 4, v_mm)
                heads(23, 24)
                scores(6)
                xm_part(0, 2)
                heads(24, 26)
                xm_part(2, 3)
                heads(26, 27)
                xm_part(3, 4)
                scores(7)
                heads(27, 29)
                if has(-1):
                    pe.wait_ge(xm_ok, i)
                    turn4(0, "xmt", lambda j: row_n[:, P * j:P * (j + 1)], xm_tr)
                heads(29, 31)
                s1_part(0, 2)
                heads(31, 32)
                s1_part(2, 4)

            run_steps(nc, pe, step, after)

        @block.vector
        def _(dve):
            V = nc.vector
            dve.wait_ge(prep_act, 1)
            V.tensor_tensor(wq_l[:, :, :], n_w[:, :, :], wq_h[:, :, :].bitcast(F32), ALU.subtract).then_inc(prep_dve, 1)
            dve.wait_ge(prep_act, 2)
            V.tensor_tensor(wk_l[:, :, :], ctx_n[:, 0, :].rearrange("p (a b) -> p a b", b=P),
                            wk_h[:, :, :].bitcast(F32), ALU.subtract).then_inc(prep_dve, 1)
            dve.wait_ge(prep_act, 3)
            V.tensor_tensor(wv_l[:, :, :], ctx_n[:, 1, :].rearrange("p (a b) -> p a b", b=P),
                            wv_h[:, :, :].bitcast(F32), ALU.subtract).then_inc(prep_dve, 1)
            dve.wait_ge(w_in[1], 48)
            dve.wait_ge(prep_pool, 1)
            V.tensor_scalar(bv_b[:, :], ones[:, :], bv_c[:, 0:1], None, ALU.mult).then_inc(prep_dve, 1)
            V.memset(half_c[:, :], -0.5).then_inc(prep_dve, 1)

            def after(i):
                if i == STEPS[0]:
                    for t in range(KT):
                        dve.wait_ge(prep_act, 3 + t + 1)
                        src = sc_ps[:, t, :] if t < SC else o_ps[:, :]
                        V.scalar_tensor_tensor(m_l[:, t, :], src, float(H) ** -0.5, m_h[:, t, :].bitcast(F32),
                                               ALU.mult, ALU.subtract).then_inc(prep_dve, 1)
                    dve.wait_ge(prep_pe, KT + 1)
                    dve.wait_ge(w_in[4], 80)
                    V.tensor_copy(bo_b[:, :], mx_ps[0:L, 0, :]).then_inc(prep_dve, 1)
                    dve.wait_ge(prep_act, 8)
                    V.tensor_tensor(wo_l[:, :, :], n_w[:, :, :], wo_h[:, :, :].bitcast(F32),
                                    ALU.subtract).then_inc(prep_dve, 1)

            def step(i, par, has):
                odd = 1 - par

                def add_mask(g):
                    if not has(0):
                        return
                    b = i
                    if g == 0:
                        dve.wait_ge(mt_in[par], ring(b, par))
                    if g == 0:
                        wait(dve, pv_mm, 2 * b)
                    if g == 4:
                        dve.wait_ge(pv_mm, 2 * b + 1)
                    dve.wait_ge(sc_mm, 24 * b + 3 * g + 1)
                    V.tensor_tensor(pr[:, g % 4, 0, :].rearrange("p (j l) -> p j l", j=J),
                                    sc_ps[:, 0, 0:JL].rearrange("p (j l) -> p j l", j=J),
                                    mask_t[par][:, 0, :].unsqueeze(1).to_broadcast([P, J, L]),
                                    ALU.add).then_inc(sc_add, 1)

                def maxima(n0, n1):
                    if not has(1):
                        return
                    b = i + 1
                    if n0 == 0:
                        dve.wait_ge(mn_in[odd], ring(b, odd))
                        wait(dve, m_tr, 2 * (b - 1))
                    for n in range(n0, n1):
                        hold(dve, a_mm, NH * b + n + 1)
                        src = mx_ps[0:L, n % 2, 0:S]
                        V.tensor_tensor_reduce(out=src, in0=src, in1=mask_n[odd][:, :], scale=1.0, scalar=-3.0e38,
                                               op0=ALU.add, op1=ALU.max,
                                               accum_out=mx[odd][:, n:n + 1]).then_inc(a_mx, 1)

                def maxima_low(b, half, w):
                    dve.wait_ge(mh_ok, 2 * b + half + 1)
                    wait(dve, m_in[half], 32 * b)
                    V.scalar_tensor_tensor(mt_l[half][:, :], work[0:16, w, 0:L], -1.0, mt_h[half][:, :].bitcast(F32),
                                           ALU.mult, ALU.subtract).then_inc(ml_ok, 1)

                if has(-2):
                    b = i - 2
                    dve.wait_ge(s1_mm, b + 1)
                    wait(dve, p1_ok, b)
                    V.tensor_reduce(nm1[:, :], work[0:L, 0, 0:S], AX.X, ALU.max, negate=True).then_inc(nm_ok, 1)
                maxima(0, 2)
                if has(0):
                    maxima_low(i, 1, 1)
                add_mask(0)
                maxima(2, 4)
                if has(-2):
                    b = i - 2
                    dve.wait_ge(p1_ok, b + 1)
                    wait(dve, ra_ok, b)
                    V.reciprocal(ra0[:, :], s1[:, :]).then_inc(ra0_ok, 1)
                    dve.wait_ge(ra0_ok, b + 1)
                    wait(dve, res_ok, b)
                    V.tensor_scalar(ra[:, :], ra0[:, :], alpha_c[:, 0:1], None, ALU.mult).then_inc(ra_ok, 1)
                maxima(4, 7)
                if has(2):
                    b = i + 2
                    dve.wait_ge(q_mm, b + 1)
                    wait(dve, q_tr, b)
                    wait(dve, xm_tr, i - 1)
                    V.tensor_tensor(row_n[:, :], work[0:L, 1, :], bq_b[:, :], ALU.add).then_inc(q_nat, 1)
                maxima(7, 8)
                add_mask(1)
                if has(-1):
                    b = i - 1
                    dve.wait_ge(dn_in, 16 * (b + 1))
                    wait(dve, rd_out, 16 * b)
                    V.reciprocal(rden[:, :], den[:, :]).then_inc(rd_ok, 1)
                maxima(8, 10)
                add_mask(2)
                maxima(10, 11)
                if has(2):
                    b = i + 2
                    dve.wait_ge(qh_ok, b + 1)
                    wait(dve, q_out, 32 * b)
                    V.scalar_tensor_tensor(x_l[:, :], work[:, 1, 0:JL], 0.25, x_h[:, :].bitcast(F32),
                                           ALU.mult, ALU.subtract).then_inc(ql_ok, 1)
                maxima(11, 13)
                if has(-1):
                    b = i - 1
                    dve.wait_ge(ot_in, 16 * (b + 1))
                    dve.wait_ge(rb_in, 16 * (b + 1))
                    V.tensor_tensor(r_b[:, :], o_l[:, :].bitcast(F32), r_b[:, :], ALU.mult).then_inc(on_ok, 1)
                if has(-2):
                    b = i - 2
                    dve.wait_ge(d_mm, b + 1)
                    dve.wait_ge(ra_ok, b + 1)
                    V.scalar_tensor_tensor(x1[par][:, :], work[0:L, 0, :], ra[:, 0:1], x1[par][:, :],
                                           ALU.mult, ALU.add).then_inc(res_ok, 1)
                if has(-1):
                    dve.wait_ge(oh_ok, i)
                    V.tensor_tensor(o_l[:, :], r_b[:, :], o_h[:, :].bitcast(F32), ALU.subtract).then_inc(ol_ok, 1)
                add_mask(3)
                maxima(13, 19)
                if has(-1):
                    b = i - 1
                    dve.wait_ge(y_mm, b + 1)
                    dve.wait_ge(xb_ok, b + 1)
                    V.tensor_tensor(y[:, :], work[0:L, 0, :], y[:, :], ALU.add).then_inc(y_ok, 1)
                    dve.wait_ge(y_ok, b + 1)
                    V.bn_stats(stats[:, :], y[:, :]).then_inc(st_ok, 1)
                    dve.wait_ge(st_ok, b + 1)
                    hold(dve, ve_ok, b)
                    V.bn_aggr(mv[:, :], stats[:, :]).then_inc(mv_ok, 1)
                if has(2):
                    b = i + 2
                    dve.wait_ge(kh_ok, b + 1)
                    wait(dve, k_out, 32 * b)
                    V.scalar_tensor_tensor(k_l[:, :], work[:, 1, 0:SP2], bk_c[:, 0:1], k_h[:, :].bitcast(F32),
                                           ALU.add, ALU.subtract).then_inc(kl_ok, 1)
                if has(-1):
                    b = i - 1
                    dve.wait_ge(rstd_ok, b + 1)
                    dve.wait_ge(mv_ok, b + 1)
                    V.tensor_scalar(y[:, :], y[:, :], mv[:, 0:1], rstd[:, 0:1],
                                    ALU.subtract, ALU.mult).then_inc(xc_ok, 1)
                maxima(19, 20)
                if has(-1):
                    b = i - 1
                    dve.wait_ge(xc_ok, b + 1)
                    if not isinstance(b, int) or b >= 2:
                        dve.wait_ge(out_ok[odd], ring(b - 2, odd))
                    V.tensor_tensor(x1[odd][:, :], y[:, :], gamma_b[:, :], ALU.mult).then_inc(xg_ok, 1)
                    dve.wait_ge(xg_ok, b + 1)
                    V.tensor_tensor(x1[odd][:, :], x1[odd][:, :], beta_b[:, :], ALU.add).then_inc(x1_ok, 1)
                add_mask(4)
                if has(1):
                    maxima_low(i + 1, 0, 0)
                maxima(20, 22)
                add_mask(5)
                if has(-1):
                    b = i - 1
                    dve.wait_ge(x1h_ok, b + 1)
                    wait(dve, xm_mm, b)
                    dve.wait_ge(q_out, 32 * upto(i + 3))
                    V.tensor_tensor(x_l[:, :], work[:, 0, 0:JL], x_h[:, :].bitcast(F32),
                                    ALU.subtract).then_inc(x1l_ok, 1)
                maxima(22, 24)
                add_mask(6)
                maxima(24, 27)
                add_mask(7)
                maxima(27, 32)

            run_steps(nc, dve, step, after)

        @block.scalar
        def _(act):
            st = pr[:, :, :, :].rearrange("p a b c -> p (a b c)")
            A = nc.scalar
            act.wait_ge(w_in[0], 48)
            A.activation(wq_h[:, :, :], n_w[:, :, :], ACT.Copy).then_inc(prep_act, 1)
            act.dma_start(st[:, 0:2048], w1q_d).then_inc(w_in[2], 16)
            act.dma_start(st[:, 2048:4096], w1k_d).then_inc(w_in[2], 16)
            act.dma_start(bo_r[:, :], bo_d).then_inc(w_in[4], 16)
            act.dma_start(gamma_b[:, :], gamma_d).then_inc(w_in[4], 16)
            act.dma_start(beta_b[:, :], beta_d).then_inc(w_in[4], 16)
            act.dma_start(alpha_c[:, :], alpha_d).then_inc(w_in[4], 16)
            A.activation(wk_h[:, :, :], ctx_n[:, 0, :].rearrange("p (a b) -> p a b", b=P),
                         ACT.Copy).then_inc(prep_act, 1)
            A.activation(wv_h[:, :, :], ctx_n[:, 1, :].rearrange("p (a b) -> p a b", b=P),
                         ACT.Copy).then_inc(prep_act, 1)
            act.wait_ge(prep_act, 1)
            act.wait_ge(prep_dve, 1)
            act.dma_start(n_w[:, :, :].rearrange("p a b -> p (a b)"), wo_d).then_inc(w_in[4], 16)

            def after(i):
                n = i - STEPS[0]
                if n == 1:
                    act.wait_ge(prep_dve, 11)
                for t in range(KT):
                    act.wait_ge(prep_pe, (KT + 1) * n + t + 1)
                    src = sc_ps[:, t, :] if t < SC else o_ps[:, :]
                    if n == 0:
                        A.activation(m_h[:, t, :], src, ACT.Copy, scale=float(H) ** -0.5).then_inc(prep_act, 1)
                    else:
                        A.activation(n_w[:, t, :], src, ACT.Copy).then_inc(prep_act, 1)
                if n == 0:
                    act.wait_ge(w_in[4], 80)
                    A.activation(wo_h[:, :, :], n_w[:, :, :], ACT.Copy).then_inc(prep_act, 1)

            def step(i, par, has):
                odd = 1 - par

                def copy_scores(g):
                    if not has(0):
                        return
                    b = i
                    act.wait_ge(sc_mm, 24 * b + 3 * g + 3)
                    if g == 0:
                        wait(act, pv_mm, 2 * b)
                    if g == 4:
                        act.wait_ge(pv_mm, 2 * b + 1)
                    A.activation(pr[:, g % 4, 1:3, :], sc_ps[:, 1:3, 0:JL], ACT.Copy).then_inc(sc_cp, 1)

                def probabilities(g):
                    if not has(0):
                        return
                    b = i
                    act.wait_ge(sc_add, 8 * b + g + 1)
                    act.wait_ge(sc_pool, 8 * b + g + 1)
                    t = pr[:, g % 4, :, :].rearrange("p c n -> p (c n)")
                    A.activation(t, t, ACT.Exp).then_inc(ex_ok, 1)

                def output(off, half):
                    if not has(off):
                        return
                    b = i + off
                    act.wait_ge(pv_mm, 2 * b + half + 1)
                    wait(act, os_out[1 - half], 16 * (b + half))
                    A.activation(o_s[:, :], o_ps[:, 0:JL], ACT.Copy).then_inc(os_ok, 1)

                def maxima_high(b, half, w):
                    act.wait_ge(m_tr, 2 * b + half + 1)
                    wait(act, m_in[half], 32 * b)
                    A.activation(mt_h[half][:, :], work[0:16, w, 0:L], ACT.Copy, scale=-1.0).then_inc(mh_ok, 1)

                if has(-2):
                    b = i - 2
                    act.wait_ge(nm_ok, b + 1)
                    wait(act, p1_tr, b)
                    wait(act, ra0_ok, b)
                    A.activation(p1[:, 0:S], work[0:L, 0, 0:S], ACT.Exp, bias=nm1[:, 0:1],
                                 accum_out=s1[:, :]).then_inc(p1_ok, 1)
                if has(0):
                    maxima_high(i, 1, 1)
                if has(2):
                    b = i + 2
                    act.wait_ge(x_in, 16 * (b + 1))
                    wait(act, q_mm, b)
                    wait(act, xl_ok, b)
                    wait(act, xm_mm, i - 1)
                    wait(act, x1l_ok, i - 1)
                    A.activation(x_h[:, :], xT[:, :], ACT.Copy).then_inc(xh_ok, 1)
                output(-1, 1)
                if has(1):
                    b = i + 1
                    act.wait_ge(v_tr, b + 1)
                    wait(act, pv_mm, 2 * (b - 1))
                    for c0, c1, k in ((0, 2, P), (2, 3, LAST)):
                        A.activation(va[odd][0:k, c0:c1, :, 0:HD].rearrange("p c g d -> p (c g) d"),
                                     work[0:k, 1, P * c0:P * c1].rearrange("p (n d) -> p n d", d=HD),
                                     ACT.Copy).then_inc(va_ok, 1)
                copy_scores(0)
                if has(-2):
                    b = i - 2
                    act.wait_ge(p1_tr, b + 1)
                    wait(act, cx_mm, b)
                    A.activation(p1_t[:, 0:2, :].rearrange("p c l -> p (c l)"), work[:, 0, 0:2 * L],
                                 ACT.Copy).then_inc(p1t_ok, 1)
                    A.activation(p1_t[0:LAST, 2, :], work[0:LAST, 0, 2 * L:3 * L], ACT.Copy).then_inc(p1t_ok, 1)
                copy_scores(1)
                probabilities(0)
                if has(2):
                    b = i + 2
                    act.wait_ge(c_in, 16 * (b + 1))
                    wait(act, v_mm, b)
                    wait(act, cl_ok, b)
                    A.activation(c_h[:, :], cT[:, :], ACT.Copy).then_inc(ch_ok, 1)
                if has(-2):
                    b = i - 2
                    act.wait_ge(cx_mm, b + 1)
                    wait(act, d_mm, b)
                    act.wait_ge(s1_mm, b + 1)
                    A.activation(turned[:, :], work[:, 0, 0:JL], ACT.Copy).then_inc(cxt_ok, 1)
                copy_scores(2)
                if has(2):
                    b = i + 2
                    act.wait_ge(q_tr, b + 1)
                    wait(act, q_out, 32 * b)
                    wait(act, ql_ok, b)
                    A.activation(x_h[:, :], work[:, 1, 0:JL], ACT.Copy, scale=0.25).then_inc(qh_ok, 1)
                if has(-1):
                    b = i - 1
                    act.wait_ge(on_ok, b + 1)
                    wait(act, y_mm, b)
                    A.activation(o_h[:, :], r_b[:, :], ACT.Copy).then_inc(oh_ok, 1)
                probabilities(1)
                copy_scores(3)
                probabilities(2)
                probabilities(3)
                if has(2):
                    b = i + 2
                    act.wait_ge(k_mm, b + 1)
                    wait(act, k_out, 32 * b)
                    wait(act, kl_ok, b)
                    A.activation(k_h[:, :], work[:, 1, 0:SP2], ACT.Identity, bias=bk_c[:, 0:1]).then_inc(kh_ok, 1)
                output(0, 0)
                copy_scores(4)
                if has(1):
                    maxima_high(i + 1, 0, 0)
                if has(-1):
                    b = i - 1
                    act.wait_ge(x1_tr, b + 1)
                    act.wait_ge(q_out, 32 * upto(i + 3))
                    wait(act, xm_mm, b)
                    A.activation(x_h[:, :], work[:, 0, 0:JL], ACT.Copy).then_inc(x1h_ok, 1)
                copy_scores(5)
                probabilities(4)
                if has(2):
                    b = i + 2
                    act.wait_ge(v_mm, b + 1)
                    wait(act, v_tr, b)
                    A.activation(vT[:, :], work[:, 1, 0:SP2], ACT.Copy).then_inc(vT_ok, 1)
                copy_scores(6)
                probabilities(5)
                if has(-1):
                    b = i - 1
                    act.wait_ge(xm_mm, b + 1)
                    wait(act, xm_tr, b)
                    act.wait_ge(q_tr, upto(i + 3))
                    A.activation(row_n[:, :], work[0:L, 0, :], ACT.Copy).then_inc(xm_ok, 1)
                copy_scores(7)
                if has(-1):
                    b = i - 1
                    act.wait_ge(xm_tr, b + 1)
                    wait(act, s1_mm, b)
                    wait(act, d_mm, b)
                    A.activation(turned[:, :], work[:, 0, 0:JL], ACT.Copy).then_inc(xmt_ok, 1)
                probabilities(6)
                probabilities(7)

            run_steps(nc, act, step, after)

        @block.gpsimd
        def _(pool):
            G = nc.gpsimd
            pool.memset(ones[:, :], 1.0).then_inc(prep_pool, 1)
            pool.memset(ident[:, :], 0.0).then_inc(prep_pool, 1)
            pool.wait_ge(prep_pool, 2)
            pool.affine_select(out=ident[:, :], in_=ident[:, :], compare_op=ALU.not_equal, fill=1.0, base=0,
                               pattern=[[-1, P]], channel_multiplier=1).then_inc(prep_pool, 1)
            for p in range(2):
                pool.wait_ge(prep_pool, 3 + 3 * p)
                pool.memset(ks[p][0:64, :, SP2:SC * P].bitcast(F32), 0.0).then_inc(prep_pool, 1)
                pool.wait_ge(prep_pool, 4 + 3 * p)
                pool.memset(va[p][:, :, :, HD:2 * HD], 1.0).then_inc(prep_pool, 1)
                pool.wait_ge(prep_pool, 5 + 3 * p)
                pool.memset(ks[p][64:66, :, 0:SC * P].bitcast(F32), 1.0).then_inc(prep_pool, 1)
            pool.wait_ge(prep_pool, 9)

            def step(i, par, has):
                odd = 1 - par

                def add_mask(g):
                    if not has(0):
                        return
                    b = i
                    if g == 0:
                        pool.wait_ge(mt_in[par], ring(b, par))
                    pool.wait_ge(sc_cp, 8 * b + g + 1)
                    t = pr[:, g % 4, 1:3, :].rearrange("p c (j l) -> p c j l", j=J)
                    G.tensor_tensor(t, t, mask_t[par][:, 1:3, :].unsqueeze(2).to_broadcast([P, 2, J, L]),
                                    ALU.add).then_inc(sc_pool, 1)

                if has(2):
                    b = i + 2
                    pool.wait_ge(xh_ok, b + 1)
                    wait(pool, q_mm, b)
                    wait(pool, xm_mm, i - 1)
                    G.tensor_tensor(x_l[:, :], xT[:, :], x_h[:, :].bitcast(F32), ALU.subtract).then_inc(xl_ok, 1)
                add_mask(0)
                if has(2):
                    b = i + 2
                    pool.wait_ge(ch_ok, b + 1)
                    wait(pool, v_mm, b)
                    G.tensor_tensor(c_l[:, :], cT[:, :], c_h[:, :].bitcast(F32), ALU.subtract).then_inc(cl_ok, 1)
                add_mask(1)
                if has(-1):
                    b = i - 1
                    pool.wait_ge(xn_in, 16 * (b + 1))
                    pool.wait_ge(prep_dve, 10)
                    G.tensor_tensor(y[:, :], y[:, :], bo_b[:, :], ALU.add).then_inc(xb_ok, 1)
                add_mask(2)
                add_mask(3)
                if has(-1):
                    b = i - 1
                    pool.wait_ge(mv_ok, b + 1)
                    hold(pool, rstd_ok, b)
                    G.tensor_scalar(ve[:, :], mv[:, 1:2], EPS, None, ALU.add).then_inc(ve_ok, 1)
                    pool.wait_ge(ve_ok, b + 1)
                    wait(pool, xc_ok, b)
                    G.tensor_tensor(rstd[:, :], ve[:, :], half_c[:, :], ALU.pow).then_inc(rstd_ok, 1)
                add_mask(4)
                add_mask(5)
                add_mask(6)
                add_mask(7)

            run_steps(nc, pool, step)


_INS = ("xT", "x", "ctxT", "ctx", "mask", "maskT", "wq", "wk", "wv", "wo", "bq", "bk", "bv", "bo",
        "gamma", "beta", "w1q", "w1k", "w1v", "w1o", "alpha")


def kernel(**inputs):
    import numpy as np
    import concourse.bacc as bacc
    from concourse.bass_utils import run_bass_kernel_spmd as run

    a = {k: np.asarray(v) for k, v in inputs.items()}

    def rows(w):
        return w.reshape(KT, P, -1).transpose(1, 0, 2).reshape(P, -1)

    def by_head(w):
        return w.reshape(-1, KVH, J, HD).transpose(0, 2, 1, 3).reshape(-1, H)

    def chunks(t, size, pieces):
        t = np.pad(t, ((0, 0), (0, size * pieces - t.shape[1]), (0, 0)))
        return t.reshape(B, pieces, size, -1).transpose(0, 2, 1, 3)

    x, c, mask = a["x"], a["ctx_2048"], a["mask_Bx1xSxS2_ff0"][:, 0]
    cT = np.pad(c.transpose(0, 2, 1), ((0, 0), (0, 0), (0, SP2 - S)))
    arrays = {
        "xT": chunks(x.transpose(0, 2, 1), P, KT).reshape(B, P, -1),
        "x": x,
        "ctxT": chunks(cT, P, KT).reshape(B, P, -1),
        "ctx": chunks(c, P, SC),
        "mask": mask,
        "maskT": chunks(mask.transpose(0, 2, 1), P, SC),
        "wq": rows(by_head(a["L0_xattn_Wq"])),
        "wk": rows(a["L0_xattn_Wk"]),
        "wv": rows(a["L0_xattn_Wv"]),
        "wo": rows(a["L0_xattn_Wo"].reshape(KVH, J, HD, H).transpose(1, 0, 2, 3).reshape(H, H)),
        "bq": np.broadcast_to(by_head(a["L0_xattn_bq"].reshape(1, H)), (L, H)),
        "bk": a["L0_xattn_bk"].reshape(P, 1),
        "bv": a["L0_xattn_bv"].reshape(P, 1),
        "bo": a["L0_xattn_bo"].reshape(1, H),
        "gamma": np.broadcast_to(a["L0_xattn_gamma"], (L, H)),
        "beta": np.broadcast_to(a["L0_xattn_beta"], (L, H)),
        "w1q": rows(a["L1_xattn_w_q"]),
        "w1k": rows(a["L1_xattn_w_k"]),
        "w1v": rows(a["L1_xattn_w_v"]),
        "w1o": rows(a["L1_xattn_w_o"].T),
        "alpha": np.broadcast_to(a["L1_xattn_alpha"].reshape(1, 1), (L, 1)),
    }
    nc = bacc.Bacc("TRN2", target_bir_lowering=False, num_devices=1)
    feeds, args = {}, []
    for name in _INS:
        t = np.ascontiguousarray(arrays[name])
        feeds[f"in_{name}"] = t
        args.append(nc.dram_tensor(f"in_{name}", t.shape, mybir.dt.from_np(t.dtype), kind="ExternalInput").ap())
    args.append(nc.dram_tensor("out", (B, L, H), F32, kind="ExternalOutput").ap())
    build(nc, *args)
    return run(nc, [feeds], core_ids=[0]).results[0]["out"]
```
